# Optimizing a Trainium2 kernel written in Bass

```python
import numpy as np
import jax
import jax.numpy as jnp

def _softmax(x, axis=-1):
    return jax.nn.softmax(x, axis=axis)

def _gelu(x):
    return jax.nn.gelu(x, approximate=True)

def _silu(x):
    return jax.nn.silu(x)

def _sigmoid(x):
    return jax.nn.sigmoid(x)

def _layernorm(x, axis=-1, eps=1e-05):
    m = jnp.mean(x, axis=axis, keepdims=True)
    v = jnp.var(x, axis=axis, keepdims=True)
    return (x - m) / jnp.sqrt(v + eps)

def _scatter_add(tgt, idx, src, axis=0):
    return tgt.at[idx].add(src)

def _segment_sum(src, seg, n):
    return jax.ops.segment_sum(src, seg, n)
kernel_name = 'mk_adaln_ffn_d1_seqx_r4_8bed85'

def setup_inputs(seed: int=0):
    np.random.seed(seed)
    _w = jnp.asarray

    def _rec_inputs():
        import jax
        import jax.numpy as jnp
        _rk = jax.random.key(seed)
        x = -0.000125 + 0.9999 * jax.random.normal(jax.random.fold_in(_rk, 1), (64, 64, 1024), jnp.float32)
        _lenS = 64 - jax.random.randint(jax.random.fold_in(_rk, 7), (64,), 0, max(1, 64 // 4) + 1, jnp.int32)
        _lenS2 = 64 - jax.random.randint(jax.random.fold_in(_rk, 8), (64,), 0, max(1, 64 // 4) + 1, jnp.int32)
        cond_128 = 0.0061147 + 1.02565 * jax.random.normal(jax.random.fold_in(_rk, 11), (64, 128), jnp.float32)
        fside_S_0 = -0.022604 + 0.987366 * jax.random.normal(jax.random.fold_in(_rk, 12), (64,), jnp.float32)
        return (x, cond_128, fside_S_0)
    x, cond_128, fside_S_0 = _rec_inputs()

    def _L0_cond_setup():
        import jax, jax.numpy as jnp
        import numpy as np
        from jax import lax
        N, C_IN, L = (32, 64, 1024)
        C_OUT, K, GROUPS = (64, 9, 4)
        C_DIM, PAD, STRIDE = (128, 4, 1)
        key = jax.random.key(seed)
        k1, k2, k3, k4, k5 = jax.random.split(key, 5)
        x = jax.random.normal(k1, (N, C_IN, L), dtype=jnp.float32)
        c = jax.random.normal(k2, (N, C_DIM), dtype=jnp.float32)
        weight = jax.random.normal(k3, (C_OUT, C_IN // GROUPS, K), dtype=jnp.float32)
        c_weight = jax.random.normal(k4, (C_OUT, C_DIM), dtype=jnp.float32)
        bias = jax.random.normal(k5, (C_OUT,), dtype=jnp.float32)
        return {'x': x, 'c': c, 'weight': weight, 'c_weight': c_weight, 'bias': bias}
    _L0_cond_all = _L0_cond_setup()
    _L0_cond_in = {k: v for k, v in _L0_cond_all.items() if k in ('weight', 'c_weight')}
    del _L0_cond_all

    def _L0_ffn_setup():
        import jax, jax.numpy as jnp
        import numpy as np
        B, T, D_IN, D_OUT = (8, 512, 1024, 1024)
        N_LORAS, RANK = (16, 32)
        SCALING = 1.0
        key = jax.random.key(seed)
        ks = jax.random.split(key, 8)
        std = 1.0 / D_IN ** 0.5
        x = jax.random.normal(ks[0], (B, T, D_IN), dtype=jnp.float32)
        idx = jax.random.randint(ks[1], (B,), 0, N_LORAS)
        gate = jax.nn.one_hot(idx, N_LORAS, dtype=jnp.float32)
        kernel = jax.random.normal(ks[2], (D_IN, D_OUT), dtype=jnp.float32) * std
        bias = jnp.zeros((D_OUT,), dtype=jnp.float32)
        lora_A = jax.random.normal(ks[3], (N_LORAS, RANK, D_IN), dtype=jnp.float32) * std
        lora_B = jax.random.normal(ks[4], (N_LORAS, D_OUT, RANK), dtype=jnp.float32) * 0.01
        lora_A_shared = jax.random.normal(ks[5], (RANK, D_IN), dtype=jnp.float32) * std
        lora_B_shared = jax.random.normal(ks[6], (D_OUT, RANK), dtype=jnp.float32) * 0.01
        return {'x': x, 'gate': gate, 'kernel': kernel, 'bias': bias, 'lora_A': lora_A, 'lora_B': lora_B, 'lora_A_shared': lora_A_shared, 'lora_B_shared': lora_B_shared}
    _L0_ffn_all = _L0_ffn_setup()
    _L0_ffn_in = {k: v for k, v in _L0_ffn_all.items() if k in ('gate', 'kernel', 'bias', 'lora_A', 'lora_B', 'lora_A_shared', 'lora_B_shared')}
    del _L0_ffn_all
    return {'x': x, 'cond_128': cond_128, 'fside_S_0': fside_S_0, 'L0_cond_weight': _L0_cond_in['weight'], 'L0_cond_c_weight': _L0_cond_in['c_weight'], 'L0_ffn_gate': _L0_ffn_in['gate'], 'L0_ffn_kernel': _L0_ffn_in['kernel'], 'L0_ffn_bias': _L0_ffn_in['bias'], 'L0_ffn_lora_A': _L0_ffn_in['lora_A'], 'L0_ffn_lora_B': _L0_ffn_in['lora_B'], 'L0_ffn_lora_A_shared': _L0_ffn_in['lora_A_shared'], 'L0_ffn_lora_B_shared': _L0_ffn_in['lora_B_shared']}

def reference(x, cond_128, fside_S_0, L0_cond_weight, L0_cond_c_weight, L0_ffn_gate, L0_ffn_kernel, L0_ffn_bias, L0_ffn_lora_A, L0_ffn_lora_B, L0_ffn_lora_A_shared, L0_ffn_lora_B_shared):
    import jax
    import jax.numpy as jnp

    def _L0_cond_ref(x, c, weight, c_weight, bias):
        import jax, jax.numpy as jnp
        import numpy as np
        from jax import lax
        N, C_IN, L = (32, 64, 1024)
        C_OUT, K, GROUPS = (64, 9, 4)
        C_DIM, PAD, STRIDE = (128, 4, 1)
        out = lax.conv_general_dilated(x, weight, window_strides=(STRIDE,), padding=[(PAD, PAD)], dimension_numbers=('NCH', 'OIH', 'NCH'), feature_group_count=GROUPS)
        ctx = jnp.einsum('nd,od->no', c, c_weight)
        out = out + ctx[:, :, None] + bias[None, :, None]
        return out

    def _L0_ffn_ref(x, gate, kernel, bias, lora_A, lora_B, lora_A_shared, lora_B_shared):
        import jax, jax.numpy as jnp
        import numpy as np
        B, T, D_IN, D_OUT = (8, 512, 1024, 1024)
        N_LORAS, RANK = (16, 32)
        SCALING = 1.0
        base_out = jnp.matmul(x, kernel) + bias
        b = gate.shape[0]
        x_flat = x.reshape(b, -1, x.shape[-1])
        A_eff = jnp.einsum('bn,nri->bri', gate, lora_A)
        B_eff = jnp.einsum('bn,nor->bor', gate, lora_B)
        Ax = jnp.einsum('bri,bti->btr', A_eff, x_flat)
        delta_flat = jnp.einsum('bor,btr->bto', B_eff, Ax)
        Ax_s = jnp.einsum('ri,bti->btr', lora_A_shared, x_flat)
        delta_flat = delta_flat + jnp.einsum('or,btr->bto', lora_B_shared, Ax_s)
        delta = delta_flat.reshape(x.shape[:-1] + (kernel.shape[-1],))
        return base_out + (SCALING * delta).astype(base_out.dtype)
    x = x + _L0_ffn_ref(_L0_cond_ref(x, cond_128, L0_cond_weight, L0_cond_c_weight, fside_S_0), L0_ffn_gate, L0_ffn_kernel, L0_ffn_bias, L0_ffn_lora_A, L0_ffn_lora_B, L0_ffn_lora_A_shared, L0_ffn_lora_B_shared)
    return x

_drawn_inputs = setup_inputs


def setup_inputs(seed=0):
    import zlib

    import numpy as np

    out = dict(_drawn_inputs(seed))
    spreads = {'L0_ffn_bias': (0.0, 0.8)}
    factors = {}
    for name, (base, spread) in spreads.items():
        noise = np.random.default_rng([zlib.crc32(name.encode()), seed]).standard_normal(out[name].shape)
        drawn = base * np.exp(spread * noise) if base else spread * noise
        out[name] = jnp.asarray(drawn.astype(out[name].dtype))
    for name, factor in factors.items():
        out[name] = (out[name] * factor).astype(out[name].dtype)
    return out
```

```python
import numpy as np
import concourse.bass as bass
from concourse import mybir
from contextlib import ExitStack

F32 = mybir.dt.float32
F32R = mybir.dt.float32r
ALU = mybir.AluOpType
ACT = mybir.ActivationFunctionType
AX = mybir.AxisListType

P = 128
NS, C, L = 64, 64, 1024
D = 1024
G, CG, TAPS = 4, 16, 9
CD = 128
NL, R = 16, 32
NB = 8
SB = NS // NB
J = 8
CL, CH = 4, 4
M = L // J
MB = M + 1
HALO = TAPS // 2
KC = 8
TT = SB * C // P
NG = SB * G
CHUNKS = 8
XSTART = [16 * c for c in range(CHUNKS)] + [MB]
XSTAGE = (XSTART[CHUNKS] - XSTART[CHUNKS - 1]) * NG
CONVS = 2 * G
CBANKS = 3
R8 = 8
RQ = R // R8


def adaln_ffn(nc, x, cond, cond_bias, conv_w, cond_w, gate, kern, bias,
              lora_a, lora_b, lora_as, lora_bs, out):
    b_scratch = nc.dram_tensor("b_scratch", [NB, 2, R, D], F32, kind="Internal").ap()

    x_v = x.rearrange("n (g ch cl) l -> (n g) ch cl l", g=G, ch=CH)
    out_v = out.rearrange("n (g ch cl) l -> (n g) ch cl l", g=G, ch=CH)
    kern_v = kern.rearrange("(ma mm jh jl) d -> jh mm ma (jl d)", ma=4, mm=32, jh=4)

    ctx = ExitStack()
    with ctx:
        def sb(name, shape, dt=F32):
            return ctx.enter_context(nc.sbuf_tensor(name, shape, dt))

        def ps(name, shape):
            return ctx.enter_context(nc.psum_tensor(name, shape, F32))

        def sem(name):
            return ctx.enter_context(nc.semaphore(name))

        def early(*specs):
            with ExitStack() as own:
                return [own.enter_context(nc.sbuf_tensor(*s)) for s in specs]

        w_hi = sb("w_hi", [P, KC, D], F32R)
        w_raw, = early(("w_raw", [P, KC, D], F32))
        w_lo = sb("w_lo", [P, KC, D], F32R)
        la, lb = early(("la", [P, RQ, L], F32), ("lb", [P, NL, J, R], F32))
        lb_ord, = early(("lb_ord", [P, J * RQ, NL, R8], F32))
        be, = early(("be", [NB * R8, RQ, 2, D], F32R))
        y_hi = sb("y_hi", [P, KC * CL * CH, NG], F32R)
        y_lo = sb("y_lo", [P, KC * CL * CH, NG], F32R)
        x_hi = sb("x_hi", [P, G, MB, SB], F32R)
        x_lo = sb("x_lo", [P, G, MB, SB], F32R)
        x_in = sb("x_in", [P, CL, L + 2 * HALO])
        la_ord, = early(("la_ord", [P, RQ, L], F32))
        lbt, = early(("lbt", [P, RQ, D], F32))
        bs_rep, = early(("bs_rep", [P, J, 4, R], F32))
        res = sb("res", [P, CL, D])
        t_hi = sb("t_hi", [P, 2, G, P], F32R)
        t_lo = sb("t_lo", [P, 2, G, P], F32R)
        x_stage = sb("x_stage", [P, 2, XSTAGE])
        as_st, bs_st = early(("as_st", [P, L], F32R), ("bs_st", [P, D], F32R))
        y_add = sb("y_add", [P, 2, 512])
        y_stage = sb("y_stage", [P, 2, 512])
        bias_rep, cond_nat, cw_nat, cond_t, cw_t = early(
            ("bias_rep", [1, G, P], F32), ("cond_nat", [NS, CD], F32), ("cw_nat", [C, CD], F32),
            ("cond_t", [CD, NS], F32), ("cw_t", [CD, C], F32))
        bias_all = sb("bias_all", [P, D])
        a_eff = sb("a_eff", [P, NB, KC, R])
        cw_rep, = early(("cw_rep", [P, G, P], F32))
        a_cur = sb("a_cur", [P, KC, 2, R], F32R)
        taps, = early(("taps", [P, C, 2 * J], F32))
        b_cur = sb("b_cur", [P, D], F32R)
        as_rep, = early(("as_rep", [P, L], F32))
        ax_st = sb("ax_st", [P, 512], F32R)
        ax_sum = sb("ax_sum", [R, 512])
        ctx_all = sb("ctx_all", [P, G, NS])
        ident = sb("ident", [P, P])
        gate_nat = sb("gate_nat", [NB, NL])
        gate_rep = sb("gate_rep", [NB, NL, R8])
        diag = sb("diag", [P, R8])
        gmix = sb("gmix", [P, NB, R8])
        ones = sb("ones", [1, NS])
        bias_nat = sb("bias_nat", [1, C])
        bs_nat = sb("bs_nat", [P, J, R])

        main = [ps(f"main{i}", [P, D]) for i in range(2)]
        conv = [ps(f"conv{i}", [P, 512]) for i in range(CBANKS)]
        rank = ps("rank", [P, 512])

        taps_zero, halo_zero, ident_ready = sem("taps_zero"), sem("halo_zero"), sem("ident_ready")
        taps_in, ctx_in, bs_in, as_in = sem("taps_in"), sem("ctx_in"), sem("bs_in"), sem("as_in")
        gate_cp = sem("gate_cp")
        gate_in, la_in, lb_in, kern_in = sem("gate_in"), sem("la_in"), sem("lb_in"), sem("kern_in")
        bias_in = sem("bias_in")
        thi_done, tlo_done = sem("thi_done"), sem("tlo_done")
        ones_done = sem("ones_done")
        ctx_tr, ctx_cp, ctx_mm, ctx_done = sem("ctx_tr"), sem("ctx_cp"), sem("ctx_mm"), sem("ctx_done")
        bs_cp, bs_tr, bs_hi, bs_lo = sem("bs_cp"), sem("bs_tr"), sem("bs_hi"), sem("bs_lo")
        as_hi, as_lo = sem("as_hi"), sem("as_lo")
        w_mm, w_sum, whi_done, wlo_done = sem("w_mm"), sem("w_sum"), sem("whi_done"), sem("wlo_done")
        diag_done, gmix_done = sem("diag_done"), sem("gmix_done")
        la_ordered, lb_ordered = sem("la_ordered"), sem("lb_ordered")
        a_mm, a_done = sem("a_mm"), sem("a_done")
        lb_tr, lbt_done, be_mm = sem("lb_tr"), sem("lbt_done"), sem("be_mm")
        be_hi, be_lo, be_out = sem("be_hi"), sem("be_lo"), sem("be_out")
        x_loaded, xt_done, xhi_done, xlo_done = sem("x_loaded"), sem("xt_done"), sem("xhi_done"), sem("xlo_done")
        conv_ready, conv_free, y_turned = sem("conv_ready"), sem("conv_free"), sem("y_turned")
        yhi_done, ylo_done = sem("yhi_done"), sem("ylo_done")
        ahi_done, acur_done, b_loaded = sem("ahi_done"), sem("acur_done"), sem("b_loaded")
        ax_ready, ax_half, ax_summed = sem("ax_ready"), sem("ax_half"), sem("ax_summed")
        axhi_done, axlo_done = sem("axhi_done"), sem("axlo_done")
        tile_done, main_free = sem("tile_done"), sem("main_free")
        res_ready = sem("res_ready")
        stored = [sem(f"stored{c}") for c in range(TT)]

        block = ctx.enter_context(nc.Block())

        def y_part(y, mh, g):
            return y[:, mh * 64:(mh + 1) * 64, :].rearrange("p q (n g) -> p q n g", g=G)[:, :, :, g]

        def y_turn(i):
            return y_stage[:, i % 2, :].rearrange("p (q n) -> p q n", n=SB)

        def x_chunk(t, c):
            m0, m1 = XSTART[c], XSTART[c + 1]
            return t[:, :, m0:m1, :].rearrange("p g m n -> p m g n")

        def x_turn(c):
            m = XSTART[c + 1] - XSTART[c]
            return x_stage[:, c % 2, 0:m * NG].rearrange("p (m n g) -> p m g n", n=SB, g=G)

        def toeplitz(t, i):
            at = (J - 1 - i % J) * CG
            return t[:, i // J, :, at:at + CG].rearrange("p g (l h) -> p g l h", h=CH)

        def toeplitz_in(i):
            return taps[:, :, i].rearrange("p (g h l) -> p g l h", g=G, h=CH)

        def bs_cols(t, h):
            return t.rearrange("q (p j) -> q j p", j=J)[:, 4 * h:4 * h + 4, :]

        def bs_turned(t):
            return t.rearrange("q (j p) -> q j p", j=4)

        def a_out(k):
            bank = (conv + [rank])[k // 2]
            return bank[:, (k % 2) * 256:(k % 2 + 1) * 256]

        def ordered(t, jl):
            return t.rearrange("p (q l h m) -> p q l h m", l=2, h=4, m=32)[:, :, jl]

        def natural(t, jl):
            return t.rearrange("p (q m h l) -> p q h m l", m=32, h=4, l=2)[:, :, :, :, jl]

        def flat(t):
            return t.rearrange("p q l -> p (q l)")

        def load_x(eng, b):
            for ch in range(CH):
                rows = x_v[bass.ds(b * NG, NG), ch, :, :]
                eng.dma_start(x_in[ch * NG:(ch + 1) * NG, :, HALO:HALO + L], rows).then_inc(x_loaded, 16)

        @block.sync
        def _(sp):
            load_x(sp, 0)
            sp.wait_ge(taps_zero, 1)
            for j in range(J):
                sp.dma_start(taps[j:P:J, :, J - 1 - j:J - 1 - j + TAPS],
                             conv_w.rearrange("o c k -> c o k")).then_inc(taps_in, 16)
            for jh in range(4):
                sp.dma_start(w_raw[jh * 32:(jh + 1) * 32, :, :].rearrange("m (a j) d -> m a (j d)", j=2),
                             kern_v[jh]).then_inc(kern_in, 16)
            for q in range(RQ):
                sp.wait_ge(be_hi, 2 * q + 2)
                sp.wait_ge(be_lo, 2 * q + 2)
                for h in range(2):
                    sp.dma_start(b_scratch[:, h, q * R8:(q + 1) * R8, :],
                                 be[:, q, h, :].bitcast(F32)).then_inc(be_out, 16)
            sp.wait_ge(be_out, 16 * 2 * RQ)

            def load_b(b):
                for q in range(4):
                    sp.dma_start(b_cur[q * R:(q + 1) * R, :].bitcast(F32).rearrange("r (a d) -> r a d", a=1),
                                 b_scratch[bass.ds(b, 1), q // 2, :, :].rearrange("a r d -> r a d")).then_inc(b_loaded, 16)

            def store(b):
                for cl in range(TT):
                    sp.wait_ge(main_free, b * TT + (cl + 3))
                    for ch in range(CH):
                        sp.dma_start(out_v[bass.ds(b * NG, NG), ch, cl, :],
                                     res[ch * NG:(ch + 1) * NG, cl, :]).then_inc(stored[cl], 16)

            sp.wait_ge(tlo_done, 2 * J)
            load_b(0)
            sp.wait_ge(res_ready, TT)
            sp.wait_ge(xt_done, CHUNKS)
            load_x(sp, 1)
            store(0)
            with sp.Fori(1, NB - 1) as b:
                sp.wait_ge(tile_done, b * TT)
                load_b(b)
                sp.wait_ge(res_ready, b * TT + TT)
                sp.wait_ge(xt_done, b * CHUNKS + CHUNKS)
                load_x(sp, b + 1)
                store(b)
            sp.wait_ge(tile_done, (NB - 1) * TT)
            load_b(NB - 1)
            store(NB - 1)
            for cl in range(TT):
                sp.wait_ge(stored[cl], 16 * CH * NB)

        @block.gpsimd
        def _(pool):
            nc.gpsimd.memset(ident[:, :], 0.0).then_inc(ident_ready, 1)
            nc.gpsimd.memset(taps[:, :, :], 0.0).then_inc(taps_zero, 1)
            pool.wait_ge(ident_ready, 1)
            nc.gpsimd.affine_select(out=ident[:, :], in_=ident[:, :], compare_op=ALU.not_equal, fill=1.0,
                                    base=0, pattern=[[-1, P]], channel_multiplier=1).then_inc(ident_ready, 1)
            nc.gpsimd.memset(x_in[:, :, 0:HALO], 0.0).then_inc(halo_zero, 1)
            nc.gpsimd.memset(x_in[:, :, HALO + L:], 0.0).then_inc(halo_zero, 1)
            nc.gpsimd.memset(ones[:, :], 1.0).then_inc(ones_done, 1)
            pool.wait_ge(lb_in, 16)
            pool.wait_ge(la_ordered, 2)
            nc.gpsimd.tensor_copy(lb_ord[:, :, :, :], lb[:, :, :, :].rearrange("p n j r -> p n (j r)")
                                  .rearrange("p n (x r) -> p x n r", r=R8)).then_inc(lb_ordered, 1)
            for k in range(KC):
                pool.wait_ge(whi_done, k + 1)
                nc.gpsimd.tensor_tensor(w_lo[:, k, :], w_raw[:, k, :], w_hi[:, k, :].bitcast(F32),
                                        ALU.subtract).then_inc(wlo_done, 1)

            def residual(b, first=False):
                pool.wait_ge(x_loaded, b * 64 + 64)
                for cl in range(TT):
                    if not first:
                        pool.wait_ge(stored[cl], b * 64)
                    nc.gpsimd.tensor_tensor(res[:, cl, :], x_in[:, cl, HALO:HALO + L], bias_all[:, :],
                                            ALU.add).then_inc(res_ready, 1)

            def batch(b, first=False):
                pool.wait_ge(ahi_done, b + 1)
                nc.gpsimd.tensor_tensor(
                    a_cur[:, :, 1, :].rearrange("p (a k) r -> p a k r", a=1),
                    a_eff[:, bass.ds(b, 1), :, :],
                    a_cur[:, :, 0, :].bitcast(F32).rearrange("p (a k) r -> p a k r", a=1),
                    ALU.subtract).then_inc(acur_done, 1)
                for i in range(CONVS):
                    mh, g = i // G, i % G
                    pool.wait_ge(yhi_done, b * CONVS + (i + 1))
                    nc.gpsimd.tensor_tensor(y_part(y_lo, mh, g), y_turn(i),
                                            y_part(y_hi, mh, g).bitcast(F32), ALU.subtract).then_inc(ylo_done, 1)
                    if i == 1:
                        residual(b, first)

            pool.wait_ge(bias_in, 16)
            pool.wait_ge(be_mm, 2 * RQ)
            batch(0, first=True)
            with pool.Fori(1, NB) as b:
                batch(b)

        @block.scalar
        def _(act):
            act.dma_start(cond_nat[:, :], cond).then_inc(ctx_in, 16)
            act.dma_start(cw_nat[:, :], cond_w).then_inc(ctx_in, 16)
            act.dma_start(bias_nat[:, :], cond_bias.rearrange("(a c) -> a c", a=1)).then_inc(ctx_in, 16)
            act.dma_start(gate_nat[:, :], gate).then_inc(gate_in, 16)
            act.dma_start(bs_nat[:, :, :], lora_bs.rearrange("(p j) r -> p j r", j=J)).then_inc(bs_in, 16)
            for q in range(4):
                act.dma_start(as_rep[q * R:(q + 1) * R, :], lora_as).then_inc(as_in, 16)
            for q in range(RQ):
                act.dma_start(la[:, q, :], lora_a[:, q * R8:(q + 1) * R8, :]).then_inc(la_in, 16)
            act.dma_start(lb[:, :, :, :].rearrange("p n j r -> p n (j r)"),
                          lora_b.rearrange("n (p j) r -> p n (j r)", j=J)).then_inc(lb_in, 16)

            def xhi(b, c):
                if c == 0 and not isinstance(b, int):
                    act.wait_ge(conv_ready, b * CONVS)
                act.wait_ge(xt_done, b * CHUNKS + (c + 1))
                nc.scalar.activation(x_chunk(x_hi, c), x_turn(c), ACT.Copy).then_inc(xhi_done, 1)

            act.wait_ge(taps_in, 16 * J)
            for i in range(2 * J):
                nc.scalar.activation(toeplitz(t_hi, i), toeplitz_in(i), ACT.Copy).then_inc(thi_done, 1)
            for c in range(CHUNKS):
                xhi(0, c)
            act.wait_ge(as_in, 64)
            for jl in range(2):
                nc.scalar.activation(ordered(as_st[:, :], jl), natural(as_rep[:, :], jl), ACT.Copy).then_inc(as_hi, 1)
            act.wait_ge(la_in, 16 * RQ)
            act.wait_ge(bs_tr, 2)
            for jl in range(2):
                nc.scalar.activation(ordered(flat(la_ord[:, :, :]), jl), natural(flat(la[:, :, :]), jl),
                                     ACT.Copy).then_inc(la_ordered, 1)
            for h in range(2):
                act.wait_ge(bs_tr, h + 1)
                nc.scalar.activation(bs_cols(bs_st[:, :], h), bs_turned(conv[1 + h][:, :]), ACT.Copy).then_inc(bs_hi, 1)
            act.wait_ge(ctx_done, 1)
            act.dma_start(bias_all[:, :], bias.partition_broadcast(P)).then_inc(bias_in, 16)
            for k in range(KC):
                act.wait_ge(w_sum, k + 1)
                nc.scalar.activation(w_hi[:, k, :], w_raw[:, k, :], ACT.Copy).then_inc(whi_done, 1)
            for k in range(KC):
                act.wait_ge(a_mm, (k | 1) + 1)
                nc.scalar.activation(a_eff[:, :, k, :].rearrange("p b (q r) -> p q b r", q=RQ),
                                     a_out(k).rearrange("p (q b r) -> p q b r", q=RQ, b=NB), ACT.Copy).then_inc(a_done, 1)
            for i in range(2 * RQ):
                act.wait_ge(be_mm, i + 1)
                nc.scalar.activation(be[:, i // 2, 0, (i % 2) * 512:(i % 2 + 1) * 512],
                                     conv[i % CBANKS][0:NB * R8, :], ACT.Copy).then_inc(be_hi, 1)

            def batch(b):
                if not isinstance(b, int):
                    act.wait_ge(ax_ready, b)
                else:
                    act.wait_ge(a_done, KC)
                nc.scalar.activation(a_cur[:, :, 0, :].rearrange("p (a k) r -> p a k r", a=1),
                                     a_eff[:, bass.ds(b, 1), :, :], ACT.Copy).then_inc(ahi_done, 1)
                if not isinstance(b, int):
                    act.wait_ge(tile_done, b * TT)
                else:
                    act.wait_ge(be_out, 16 * 2 * RQ)
                for i in range(CONVS):
                    act.wait_ge(y_turned, b * CONVS + (i + 1))
                    nc.scalar.activation(y_part(y_hi, i // G, i % G), y_turn(i), ACT.Copy).then_inc(yhi_done, 1)
                act.wait_ge(ax_ready, b + 1)
                nc.scalar.activation(ax_sum[:, :], rank[R:2 * R, :], ACT.Copy).then_inc(ax_half, 1)
                act.wait_ge(ax_summed, b + 1)
                for q in (0, 2):
                    nc.scalar.activation(ax_st[q * R:(q + 1) * R, :], ax_sum[:, :], ACT.Copy).then_inc(axhi_done, 1)

            batch(0)
            with act.Fori(1, NB) as b:
                for c in range(CHUNKS):
                    xhi(b, c)
                batch(b)

        @block.vector
        def _(dve):
            dve.sem_inc(main_free, 2)
            dve.sem_inc(conv_free, CONVS)

            def xturn(b, c):
                if c == 0:
                    dve.wait_ge(x_loaded, b * 64 + 64)
                if c >= 2:
                    dve.wait_ge(xlo_done, b * CHUNKS + (c - 1))
                elif not isinstance(b, int):
                    dve.wait_ge(xlo_done, b * CHUNKS)
                m = XSTART[c + 1] - XSTART[c]
                blocks = x_in[:, :, :].rearrange("p c (m j) -> p m c j", j=J)[:, XSTART[c]:XSTART[c + 1]]
                nc.vector.transpose(x_stage[:, c % 2, 0:m * NG].rearrange("p (m s) -> p m s", s=NG),
                                    blocks).then_inc(xt_done, 1)

            def xlo(b, c):
                dve.wait_ge(xhi_done, b * CHUNKS + (c + 1))
                nc.vector.tensor_tensor(x_chunk(x_lo, c), x_turn(c), x_chunk(x_hi, c).bitcast(F32),
                                        ALU.subtract).then_inc(xlo_done, 1)

            def x_steps(b, c0, c1):
                for c in range(c0, c1):
                    xturn(b, c)
                    if c > c0:
                        xlo(b, c - 1)
                xlo(b, c1 - 1)

            def y_steps(b):
                def turn(i):
                    if i >= 2:
                        dve.wait_ge(ylo_done, b * CONVS + (i - 1))
                    elif not isinstance(b, int):
                        dve.wait_ge(ylo_done, b * CONVS + (i - 1))
                    dve.wait_ge(conv_free, b * CONVS + (i + 1 + CONVS))
                    src = y_add[:, i % 2, :].rearrange("p (a m n) -> p a n m", a=2, n=SB)
                    dst = y_stage[:, i % 2, :].rearrange("p (a q n) -> p a n q", a=2, n=SB)
                    nc.vector.transpose(dst, src).then_inc(y_turned, 1)

                for i in range(CONVS):
                    g = i % G
                    dve.wait_ge(conv_ready, b * CONVS + (i + 1))
                    if i >= 2:
                        dve.wait_ge(y_turned, b * CONVS + (i - 1))
                    elif not isinstance(b, int):
                        dve.wait_ge(y_turned, b * CONVS + (i - 1))
                    term = ctx_all[:, g, bass.ds(b * SB, SB)].unsqueeze(1).broadcast_to([P, 64, SB])
                    nc.vector.tensor_tensor(y_add[:, i % 2, :].rearrange("p (m n) -> p m n", n=SB),
                                            conv[i % CBANKS][:, :].rearrange("p (m n) -> p m n", n=SB),
                                            term, ALU.add).then_inc(conv_free, 1)
                    if i >= 1:
                        turn(i - 1)
                turn(CONVS - 1)

            def ax_steps(b):
                dve.wait_ge(ax_half, b + 1)
                nc.vector.tensor_tensor(ax_sum[:, :], rank[0:R, :], ax_sum[:, :], ALU.add).then_inc(ax_summed, 1)
                dve.wait_ge(axhi_done, b * 2 + 2)
                for q in (1, 3):
                    nc.vector.tensor_tensor(ax_st[q * R:(q + 1) * R, :], ax_sum[:, :],
                                            ax_st[0:R, :].bitcast(F32), ALU.subtract).then_inc(axlo_done, 1)

            def finish(b, cl):
                dve.wait_ge(tile_done, b * TT + (cl + 1))
                dve.wait_ge(res_ready, b * TT + (cl + 1))
                nc.vector.tensor_tensor(res[:, cl, :], main[cl % 2][:, :], res[:, cl, :],
                                        ALU.add).then_inc(main_free, 1)

            dve.wait_ge(gate_in, 16)
            nc.vector.tensor_copy(gate_rep[:, :, :], gate_nat[:, :].unsqueeze(2).broadcast_to([NB, NL, R8])).then_inc(gate_cp, 1)
            dve.wait_ge(ctx_tr, 1)
            nc.vector.tensor_copy(cond_t[:, :], rank[:, 0:NS]).then_inc(ctx_cp, 1)
            for g in range(G):
                nc.vector.tensor_copy(
                    cw_rep[:, g, :].rearrange("p (j l h) -> p j l h", j=J, l=CL),
                    rank[:, NS + g * CG:NS + (g + 1) * CG].rearrange("p (h l) -> p l h", l=CL)
                    .unsqueeze(1).broadcast_to([P, J, CL, CH])).then_inc(ctx_cp, 1)
                nc.vector.tensor_copy(
                    bias_rep[:, g, :].rearrange("p (j l h) -> p j l h", j=J, l=CL),
                    bias_nat[:, g * CG:(g + 1) * CG].rearrange("p (h l) -> p l h", l=CL)
                    .unsqueeze(1).broadcast_to([1, J, CL, CH])).then_inc(ctx_cp, 1)
            dve.wait_ge(ctx_mm, 1)
            nc.vector.tensor_copy(ctx_all[:, :, :].rearrange("p g n -> p (g n)"), conv[0][:, 0:G * NS]).then_inc(ctx_done, 1)
            dve.wait_ge(bs_in, 16)
            nc.vector.tensor_copy(bs_rep[:, :, :, :], bs_nat[:, :, :].unsqueeze(2).broadcast_to([P, J, 4, R])).then_inc(bs_cp, 1)
            dve.wait_ge(ident_ready, 2)
            nc.vector.tensor_reduce(diag[:, :], ident[:, :].rearrange("p (n r) -> p r n", r=R8), AX.X, ALU.add).then_inc(diag_done, 1)
            dve.wait_ge(diag_done, 1)
            nc.vector.tensor_tensor(gmix[:, :, :], diag[:, :].unsqueeze(1).broadcast_to([P, NB, R8]),
                                    rank[:, P:P + NB].unsqueeze(2).broadcast_to([P, NB, R8]), ALU.mult).then_inc(gmix_done, 1)
            for i in range(2 * J):
                dve.wait_ge(thi_done, i + 1)
                nc.vector.tensor_tensor(toeplitz(t_lo, i), toeplitz_in(i), toeplitz(t_hi, i).bitcast(F32),
                                        ALU.subtract).then_inc(tlo_done, 1)
            dve.wait_ge(halo_zero, 2)
            x_steps(0, 0, CHUNKS)
            for jl in range(2):
                dve.wait_ge(as_hi, jl + 1)
                nc.vector.tensor_tensor(ordered(as_st[64:P, :], jl), natural(as_rep[64:P, :], jl),
                                        ordered(as_st[64:P, :], jl).bitcast(F32), ALU.subtract).then_inc(as_lo, 1)
            for h in range(2):
                dve.wait_ge(bs_hi, h + 1)
                for q in (1, 3):
                    rows = slice(q * R, (q + 1) * R)
                    nc.vector.tensor_tensor(bs_cols(bs_st[rows, :], h), bs_turned(conv[1 + h][rows, :]),
                                            bs_cols(bs_st[rows, :], h).bitcast(F32), ALU.subtract).then_inc(bs_lo, 1)
            dve.wait_ge(kern_in, 64)
            for k in range(KC):
                dve.wait_ge(w_mm, k + 1)
                nc.vector.tensor_tensor(w_raw[:, k, :], main[k % 2][:, :], w_raw[:, k, :], ALU.add).then_inc(w_sum, 1)
            for q in range(RQ):
                dve.wait_ge(lb_tr, q + 1)
                nc.vector.tensor_copy(lbt[:, q, :].rearrange("s (p j) -> s j p", j=J),
                                      main[q % 2][:, :].rearrange("s (j p) -> s j p", j=J)).then_inc(lbt_done, 1)
            for i in range(2 * RQ):
                dve.wait_ge(be_hi, i + 1)
                half = slice((i % 2) * 512, (i % 2 + 1) * 512)
                nc.vector.tensor_tensor(be[:, i // 2, 1, half], conv[i % CBANKS][0:NB * R8, :],
                                        be[:, i // 2, 0, half].bitcast(F32), ALU.subtract).then_inc(be_lo, 1)

            y_steps(0)
            ax_steps(0)
            with dve.Fori(1, NB) as b:
                finish(b - 1, 0)
                x_steps(b, 0, 3)
                finish(b - 1, 1)
                x_steps(b, 3, 6)
                finish(b - 1, 2)
                x_steps(b, 6, CHUNKS)
                finish(b - 1, 3)
                y_steps(b)
                ax_steps(b)
            for cl in range(TT):
                finish(NB - 1, cl)

        @block.tensor
        def _(pe):
            mm = nc.tensor.matmul

            pe.wait_ge(ident_ready, 2)
            pe.wait_ge(ctx_in, 48)
            pe.wait_ge(gate_cp, 1)
            mm(rank[:, P:P + NB], gate_rep[:, :, :].rearrange("b n r -> b (n r)"), ident[0:NB, 0:NB],
               start=True, stop=True)
            nc.tensor.transpose(rank[:, 0:NS], cond_nat[:, :], ident[0:NS, 0:NS])
            nc.tensor.transpose(rank[:, NS:NS + C], cw_nat[:, :], ident[0:C, 0:C]).then_inc(ctx_tr, 1)
            pe.wait_ge(ctx_cp, 1 + 2 * G)
            pe.wait_ge(ones_done, 1)
            for g in range(G):
                mm(conv[0][:, g * NS:(g + 1) * NS], cw_rep[:, g, :], cond_t[:, :], start=True, stop=False)
                last = mm(conv[0][:, g * NS:(g + 1) * NS], bias_rep[:, g, :], ones[:, :], start=False, stop=True)
            last.then_inc(ctx_mm, 1)
            pe.wait_ge(bs_cp, 1)
            for j in range(J):
                t = nc.tensor.transpose(conv[1 + j // 4][:, (j % 4) * P:(j % 4 + 1) * P],
                                        bs_rep[:, j, :, :].rearrange("p a r -> p (a r)"), ident[:, :])
                if j % 4 == 3:
                    t.then_inc(bs_tr, 1)
            pe.wait_ge(as_lo, 2)
            pe.wait_ge(bs_lo, 4)
            for k in range(KC):
                if k >= 2:
                    pe.wait_ge(w_sum, k - 1)
                rows = as_st[:, k * P:(k + 1) * P]
                for h in range(2):
                    last = mm(main[k % 2][:, h * 512:(h + 1) * 512], rows, bs_st[:, h * 512:(h + 1) * 512],
                              start=True, stop=True)
                last.then_inc(w_mm, 1)
            pe.wait_ge(la_ordered, 2)
            pe.wait_ge(gmix_done, 1)
            pe.wait_ge(ctx_done, 1)
            for k in range(KC):
                for q in range(RQ):
                    last = mm(a_out(k)[:, q * 64:(q + 1) * 64], la_ord[:, q, k * P:(k + 1) * P],
                              gmix[:, :, :].rearrange("p b r -> p (b r)"), start=True, stop=True)
                last.then_inc(a_mm, 1)
            pe.wait_ge(lb_ordered, 1)
            for q in range(RQ):
                pe.wait_ge(w_sum, KC)
                if q >= 2:
                    pe.wait_ge(lbt_done, q - 1)
                for j in range(J):
                    t = nc.tensor.transpose(main[q % 2][:, j * P:(j + 1) * P],
                                            lb_ord[:, j * RQ + q, :, :].rearrange("p n r -> p (n r)"), ident[:, :])
                t.then_inc(lb_tr, 1)
            pe.wait_ge(a_done, KC)
            for i in range(2 * RQ):
                q, h = i // 2, i % 2
                pe.wait_ge(lbt_done, q + 1)
                if i >= CBANKS:
                    pe.wait_ge(be_lo, i - CBANKS + 1)
                mm(conv[i % CBANKS][0:NB * R8, :], gmix[:, :, :].rearrange("p b r -> p (b r)"),
                   lbt[:, q, h * 512:(h + 1) * 512], start=True, stop=True).then_inc(be_mm, 1)
            pe.wait_ge(be_lo, 2 * RQ)
            pe.wait_ge(lbt_done, RQ)
            pe.wait_ge(wlo_done, KC)

            def dense(b, cl, k):
                cols = slice(k * CL + cl, k * CL + cl + 1)
                yh = y_hi[:, (k * CL + cl) * CH:(k * CL + cl + 1) * CH, :].rearrange("p h s -> p (h s)")
                yl = y_lo[:, (k * CL + cl) * CH:(k * CL + cl + 1) * CH, :].rearrange("p h s -> p (h s)")
                for lhs, rhs, first in ((yh, w_hi, True), (yh, w_lo, False), (yl, w_hi, False)):
                    for h in range(2):
                        mm(main[cl % 2][:, h * 512:(h + 1) * 512], lhs, rhs[:, k, h * 512:(h + 1) * 512],
                           start=k == 0 and first, stop=False)

            with pe.Fori(0, NB) as b:
                pe.wait_ge(xlo_done, b * CHUNKS + CHUNKS)
                for i in range(CONVS):
                    mh, g = i // G, i % G
                    before = i - CBANKS if i >= CBANKS else (6, 7, 5)[i] - CONVS
                    pe.wait_ge(conv_free, b * CONVS + (before + 1 + CONVS))
                    n = 0
                    for w in range(2):
                        rows = slice(mh * 64 + w, mh * 64 + w + 64)
                        for lhs, rhs in ((t_hi, x_hi), (t_hi, x_lo), (t_lo, x_hi)):
                            last = mm(conv[i % CBANKS][:, :], lhs[:, w, g, :],
                                      rhs[:, g, rows, :].rearrange("p m n -> p (m n)"), start=n == 0, stop=n == 5)
                            n += 1
                    last.then_inc(conv_ready, 1)
                for cl in range(TT):
                    pe.wait_ge(main_free, b * TT + (cl + 1))
                    for k in range(KC):
                        if cl == 0 and k == 0:
                            pe.wait_ge(ylo_done, b * CONVS + G)
                        if cl == 0 and k == 4:
                            pe.wait_ge(ylo_done, b * CONVS + CONVS)
                            pe.wait_ge(acur_done, b + 1)
                            for kk in range(KC):
                                lhs = a_cur[:, kk, :, :].rearrange("p a r -> p (a r)")
                                for y in (y_hi, y_lo):
                                    last = mm(rank[0:2 * R, :], lhs,
                                              y[:, kk * 16:(kk + 1) * 16, :].rearrange("p q s -> p (q s)"),
                                              start=kk == 0 and y is y_hi, stop=kk == KC - 1 and y is y_lo)
                            last.then_inc(ax_ready, 1)
                        dense(b, cl, k)
                    if cl == 0:
                        pe.wait_ge(axlo_done, b * 2 + 2)
                        pe.wait_ge(b_loaded, b * 64 + 64)
                    for h in range(2):
                        last = mm(main[cl % 2][:, h * 512:(h + 1) * 512], ax_st[:, cl * P:(cl + 1) * P],
                                  b_cur[:, h * 512:(h + 1) * 512], start=False, stop=True)
                    last.then_inc(tile_done, 1)


_INS = ['x', 'cond_128', 'fside_S_0', 'L0_cond_weight', 'L0_cond_c_weight', 'L0_ffn_gate', 'L0_ffn_kernel',
        'L0_ffn_bias', 'L0_ffn_lora_A', 'L0_ffn_lora_B', 'L0_ffn_lora_A_shared', 'L0_ffn_lora_B_shared']


def kernel(**inputs):
    import concourse.bacc as bacc
    from concourse.bass_utils import run_bass_kernel_spmd

    nc = bacc.Bacc("TRN2", target_bir_lowering=False, num_devices=1)
    arrays, args = {}, []
    for name in _INS:
        a = np.ascontiguousarray(inputs[name])
        arrays[f"in_{name}"] = a
        args.append(nc.dram_tensor(f"in_{name}", a.shape, mybir.dt.from_np(a.dtype), kind="ExternalInput").ap())
    args.append(nc.dram_tensor("out", (NS, C, L), F32, kind="ExternalOutput").ap())
    adaln_ffn(nc, *args)
    r = run_bass_kernel_spmd(nc, [arrays], core_ids=[0])
    return r.results[0]["out"]
```

```python
import numpy as np
import concourse.bass as bass
from concourse import mybir
from contextlib import ExitStack

F32 = mybir.dt.float32
F32R = mybir.dt.float32r
ALU = mybir.AluOpType
ACT = mybir.ActivationFunctionType
AX = mybir.AxisListType

P = 128
NS, C, L = 64, 64, 1024
D = 1024
G, CG, TAPS = 4, 16, 9
CD = 128
NL, R = 16, 32
NB = 8
SB = NS // NB
J = 8
CL, CH = 4, 4
M = L // J
MB = M + 1
HALO = TAPS // 2
KC = 8
TT = SB * C // P
NG = SB * G
CHUNKS = 8
XSTART = [16 * c for c in range(CHUNKS)] + [MB]
XSTAGE = (XSTART[CHUNKS] - XSTART[CHUNKS - 1]) * NG
CONVS = 2 * G
CBANKS = 3
R8 = 8
RQ = R // R8


def adaln_ffn(nc, x, cond, cond_bias, conv_w, cond_w, gate, kern, bias,
              lora_a, lora_b, lora_as, lora_bs, out):
    b_scratch = nc.dram_tensor("b_scratch", [NB, 2, R, D], F32, kind="Internal").ap()

    x_v = x.rearrange("n (g ch cl) l -> (n g) ch cl l", g=G, ch=CH)
    out_v = out.rearrange("n (g ch cl) l -> (n g) ch cl l", g=G, ch=CH)
    kern_v = kern.rearrange("(ma mm jh jl) d -> jh mm ma (jl d)", ma=4, mm=32, jh=4)

    ctx = ExitStack()
    with ctx:
        def sb(name, shape, dt=F32):
            return ctx.enter_context(nc.sbuf_tensor(name, shape, dt))

        def ps(name, shape):
            return ctx.enter_context(nc.psum_tensor(name, shape, F32))

        def sem(name):
            return ctx.enter_context(nc.semaphore(name))

        def early(*specs):
            with ExitStack() as own:
                return [own.enter_context(nc.sbuf_tensor(*s)) for s in specs]

        la, lb = early(("la", [P, RQ, L], F32), ("lb", [P, NL, J, R], F32))
        lb_ord, be = early(("lb_ord", [P, J * RQ, NL, R8], F32), ("be", [P, RQ, D], F32R))
        w_hi = sb("w_hi", [P, KC, D], F32R)
        w_raw, = early(("w_raw", [P, KC, D], F32))
        w_lo = sb("w_lo", [P, KC, D], F32R)
        y_hi = sb("y_hi", [P, KC * CL * CH, NG], F32R)
        y_lo = sb("y_lo", [P, KC * CL * CH, NG], F32R)
        x_hi = sb("x_hi", [P, G, MB, SB], F32R)
        x_lo = sb("x_lo", [P, G, MB, SB], F32R)
        x_in = sb("x_in", [P, CL, L + 2 * HALO])
        bs_rep, = early(("bs_rep", [P, J, 4, R], F32))
        la_ord, = early(("la_ord", [P, RQ, L], F32))
        lbt, = early(("lbt", [P, RQ, D], F32))
        res = sb("res", [P, CL, D])
        t_hi = sb("t_hi", [P, 2, G, P], F32R)
        t_lo = sb("t_lo", [P, 2, G, P], F32R)
        x_stage = sb("x_stage", [P, 2, XSTAGE])
        y_add = sb("y_add", [P, 2, 512])
        y_stage = sb("y_stage", [P, 2, 512])
        as_st, = early(("as_st", [P, L], F32R))
        bias_all = sb("bias_all", [P, D])
        bias_rep, cond_nat, cw_nat, cond_t, cw_rep = early(
            ("bias_rep", [1, G, P], F32), ("cond_nat", [NS, CD], F32), ("cw_nat", [C, CD], F32),
            ("cond_t", [CD, NS], F32), ("cw_rep", [P, G, P], F32))
        a_eff = sb("a_eff", [P, NB, KC, R])
        taps, = early(("taps", [P, C, 2 * J], F32))
        b_cur = sb("b_cur", [P, D], F32R)
        as_rep, = early(("as_rep", [P, L], F32))
        ax_st = sb("ax_st", [P, 512], F32R)
        ax_sum = sb("ax_sum", [R, 512])
        bs_st, = early(("bs_st", [P, D], F32R))
        a_cur = sb("a_cur", [P, KC, 2, R], F32R)
        bs_nat = sb("bs_nat", [P, J, R])
        sb("bs_st_rest", [P, 256])
        ctx_all = sb("ctx_all", [P, G, NS])
        ident = sb("ident", [P, P])
        gate_nat = sb("gate_nat", [NB, NL])
        gate_rep = sb("gate_rep", [NB, NL, R8])
        diag = sb("diag", [P, R8])
        gmix = sb("gmix", [P, NB, R8])
        ones = sb("ones", [1, NS])
        bias_nat = sb("bias_nat", [1, C])

        main = [ps(f"main{i}", [P, D]) for i in range(2)]
        conv = [ps(f"conv{i}", [P, 512]) for i in range(CBANKS)]
        rank = ps("rank", [P, 512])

        taps_zero, halo_zero, ident_ready = sem("taps_zero"), sem("halo_zero"), sem("ident_ready")
        taps_in, ctx_in, bs_in, as_in = sem("taps_in"), sem("ctx_in"), sem("bs_in"), sem("as_in")
        gate_cp = sem("gate_cp")
        gate_in, la_in, lb_in = sem("gate_in"), sem("la_in"), sem("lb_in")
        kern_in = [sem(f"kern_in{i}") for i in range(2)]
        bias_in = sem("bias_in")
        thi_done, tlo_done = sem("thi_done"), sem("tlo_done")
        ones_done = sem("ones_done")
        ctx_tr, ctx_cp, ctx_mm, ctx_done = sem("ctx_tr"), sem("ctx_cp"), sem("ctx_mm"), sem("ctx_done")
        bs_cp, bs_tr, bs_hi, bs_lo = sem("bs_cp"), sem("bs_tr"), sem("bs_hi"), sem("bs_lo")
        as_hi, as_lo = sem("as_hi"), sem("as_lo")
        w_mm, w_sum, whi_done, wlo_done = sem("w_mm"), sem("w_sum"), sem("whi_done"), [sem(f"wlo_done{i}") for i in range(2)]
        diag_done, gmix_done = sem("diag_done"), sem("gmix_done")
        la_ordered, lb_ordered = sem("la_ordered"), sem("lb_ordered")
        a_mm, a_done = sem("a_mm"), sem("a_done")
        lb_tr, lbt_done, be_mm = sem("lb_tr"), sem("lbt_done"), sem("be_mm")
        be_hi, be_lo, be_out = sem("be_hi"), sem("be_lo"), sem("be_out")
        x_first = [sem(f"x_first{i}") for i in range(2)]
        x_loaded, xt_done, xhi_done, xlo_done = sem("x_loaded"), sem("xt_done"), sem("xhi_done"), sem("xlo_done")
        conv_ready, conv_free, y_turned = sem("conv_ready"), sem("conv_free"), sem("y_turned")
        yhi_done, ylo_done = sem("yhi_done"), sem("ylo_done")
        ahi_done, acur_done, b_loaded = sem("ahi_done"), sem("acur_done"), sem("b_loaded")
        ax_ready, ax_half, ax_summed = sem("ax_ready"), sem("ax_half"), sem("ax_summed")
        axhi_done, axlo_done = sem("axhi_done"), sem("axlo_done")
        tile_done, main_free = sem("tile_done"), sem("main_free")
        res_ready = sem("res_ready")
        stored = [sem(f"stored{c}") for c in range(TT)]

        block = ctx.enter_context(nc.Block())

        def y_part(y, mh, g):
            return y[:, mh * 64:(mh + 1) * 64, :].rearrange("p q (n g) -> p q n g", g=G)[:, :, :, g]

        def y_turn(i):
            return y_stage[:, i % 2, :].rearrange("p (q n) -> p q n", n=SB)

        def x_chunk(t, c):
            m0, m1 = XSTART[c], XSTART[c + 1]
            return t[:, :, m0:m1, :].rearrange("p g m n -> p m g n")

        def x_turn(c):
            m = XSTART[c + 1] - XSTART[c]
            return x_stage[:, c % 2, 0:m * NG].rearrange("p (m n g) -> p m g n", n=SB, g=G)

        def toeplitz(t, i):
            at = (J - 1 - i % J) * CG
            return t[:, i // J, :, at:at + CG].rearrange("p g (l h) -> p g l h", h=CH)

        def toeplitz_in(i):
            return taps[:, :, i].rearrange("p (g h l) -> p g l h", g=G, h=CH)

        def bs_cols(t, h):
            return t.rearrange("q (p j) -> q j p", j=J)[:, 4 * h:4 * h + 4, :]

        def bs_turned(t, h):
            return t[:, h * 512:(h + 1) * 512].rearrange("q (j p) -> q j p", j=4)

        def a_out(k):
            return main[k // 4][:, (k % 4) * 256:(k % 4 + 1) * 256]

        def ordered(t, jl):
            return t.rearrange("p (q l h m) -> p q l h m", l=2, h=4, m=32)[:, :, jl]

        def natural(t, jl):
            return t.rearrange("p (q m h l) -> p q h m l", m=32, h=4, l=2)[:, :, :, :, jl]

        def flat(t):
            return t.rearrange("p q l -> p (q l)")

        def load_x(eng, b):
            for ch in range(CH):
                rows = x_v[bass.ds(b * NG, NG), ch, :, :]
                eng.dma_start(x_in[ch * NG:(ch + 1) * NG, :, HALO:HALO + L], rows).then_inc(x_loaded, 16)

        @block.sync
        def _(sp):
            for half in range(2):
                at = half * L // 2
                for ch in range(CH):
                    sp.dma_start(x_in[ch * NG:(ch + 1) * NG, :, HALO + at:HALO + at + L // 2],
                                 x_v[0:NG, ch, :, at:at + L // 2]).then_inc(x_first[half], 16)
            sp.dma_start(bs_nat[:, :, :], lora_bs.rearrange("(p j) r -> p j r", j=J)).then_inc(bs_in, 16)
            for q in range(4):
                sp.dma_start(as_rep[q * R:(q + 1) * R, :], lora_as).then_inc(as_in, 16)
            for q in range(RQ):
                sp.dma_start(la[:, q, :], lora_a[:, q * R8:(q + 1) * R8, :]).then_inc(la_in, 16)
            for half in range(2):
                for jh in range(4):
                    sp.dma_start(w_raw[jh * 32:(jh + 1) * 32, half * 4:(half + 1) * 4, :]
                                 .rearrange("m (a j) d -> m a (j d)", j=2),
                                 kern_v[jh, :, half * 2:(half + 1) * 2]).then_inc(kern_in[half], 16)
                if half == 0:
                    sp.dma_start(lb[:, :, :, :].rearrange("p n j r -> p n (j r)"),
                                 lora_b.rearrange("n (p j) r -> p n (j r)", j=J)).then_inc(lb_in, 16)
            sp.wait_ge(w_mm, KC)
            sp.dma_start(bias_all[:, :], bias.partition_broadcast(P)).then_inc(bias_in, 16)
            for q in range(RQ):
                sp.wait_ge(be_hi, 2 * q + 2)
                sp.wait_ge(be_lo, 2 * q + 2)
                for h in range(2):
                    sp.dma_start(b_scratch[:, h, q * R8:(q + 1) * R8, :],
                                 be[h * 64:(h + 1) * 64, q, :].bitcast(F32)).then_inc(be_out, 16)
            sp.wait_ge(be_out, 16 * 2 * RQ)

            def load_b(b):
                for q in range(4):
                    sp.dma_start(b_cur[q * R:(q + 1) * R, :].bitcast(F32).rearrange("r (a d) -> r a d", a=1),
                                 b_scratch[bass.ds(b, 1), q // 2, :, :].rearrange("a r d -> r a d")).then_inc(b_loaded, 16)

            def store(b):
                for cl in range(TT):
                    sp.wait_ge(main_free, b * TT + (cl + 3))
                    for ch in range(CH):
                        sp.dma_start(out_v[bass.ds(b * NG, NG), ch, cl, :],
                                     res[ch * NG:(ch + 1) * NG, cl, :]).then_inc(stored[cl], 16)

            sp.wait_ge(tlo_done, 2 * J)
            load_b(0)
            sp.wait_ge(res_ready, TT)
            sp.wait_ge(xt_done, CHUNKS)
            load_x(sp, 1)
            store(0)
            with sp.Fori(1, NB - 1) as b:
                sp.wait_ge(tile_done, b * TT)
                load_b(b)
                sp.wait_ge(res_ready, b * TT + TT)
                sp.wait_ge(xt_done, b * CHUNKS + CHUNKS)
                load_x(sp, b + 1)
                store(b)
            sp.wait_ge(tile_done, (NB - 1) * TT)
            load_b(NB - 1)
            store(NB - 1)
            for cl in range(TT):
                sp.wait_ge(stored[cl], 16 * CH * NB)

        @block.gpsimd
        def _(pool):
            nc.gpsimd.memset(ident[:, :], 0.0).then_inc(ident_ready, 1)
            nc.gpsimd.memset(x_in[:, :, 0:HALO], 0.0).then_inc(halo_zero, 1)
            nc.gpsimd.memset(x_in[:, :, HALO + L:], 0.0).then_inc(halo_zero, 1)
            nc.gpsimd.memset(ones[:, :], 1.0).then_inc(ones_done, 1)
            pool.wait_ge(ident_ready, 1)
            nc.gpsimd.affine_select(out=ident[:, :], in_=ident[:, :], compare_op=ALU.not_equal, fill=1.0,
                                    base=0, pattern=[[-1, P]], channel_multiplier=1).then_inc(ident_ready, 1)
            for c in range(CHUNKS):
                pool.wait_ge(xhi_done, c + 1)
                nc.gpsimd.tensor_tensor(x_chunk(x_lo, c), x_turn(c), x_chunk(x_hi, c).bitcast(F32),
                                        ALU.subtract).then_inc(xlo_done, 1)

            def a_lo(b):
                pool.wait_ge(ahi_done, b + 1)
                nc.gpsimd.tensor_tensor(
                    a_cur[:, :, 1, :].rearrange("p (a k) r -> p a k r", a=1),
                    a_eff[:, bass.ds(b, 1), :, :],
                    a_cur[:, :, 0, :].bitcast(F32).rearrange("p (a k) r -> p a k r", a=1),
                    ALU.subtract).then_inc(acur_done, 1)

            def y_los(b):
                for i in range(CONVS):
                    mh, g = i // G, i % G
                    pool.wait_ge(yhi_done, b * CONVS + (i + 1))
                    nc.gpsimd.tensor_tensor(y_part(y_lo, mh, g), y_turn(i),
                                            y_part(y_hi, mh, g).bitcast(F32), ALU.subtract).then_inc(ylo_done, 1)

            def residual(cl):
                nc.gpsimd.tensor_tensor(res[:, cl, :], x_in[:, cl, HALO:HALO + L], bias_all[:, :],
                                        ALU.add).then_inc(res_ready, 1)

            y_los(0)
            for k in range(0, KC, 2):
                pool.wait_ge(whi_done, k + 1)
                nc.gpsimd.tensor_tensor(w_lo[:, k, :], w_raw[:, k, :], w_hi[:, k, :].bitcast(F32),
                                        ALU.subtract).then_inc(wlo_done[0], 1)
            a_lo(0)
            pool.wait_ge(bias_in, 16)
            pool.wait_ge(be_mm, 2 * RQ)
            for cl in range(TT):
                residual(cl)
            with pool.Fori(1, NB) as b:
                a_lo(b)
                y_los(b)
                pool.wait_ge(x_loaded, b * 64)
                for cl in range(TT):
                    pool.wait_ge(stored[cl], b * 64)
                    residual(cl)

        @block.scalar
        def _(act):
            act.dma_start(cond_nat[:, :], cond).then_inc(ctx_in, 16)
            act.dma_start(cw_nat[:, :], cond_w).then_inc(ctx_in, 16)
            act.dma_start(bias_nat[:, :], cond_bias.rearrange("(a c) -> a c", a=1)).then_inc(ctx_in, 16)
            act.dma_start(gate_nat[:, :], gate).then_inc(gate_in, 16)
            act.wait_ge(taps_zero, 1)
            for j in range(J):
                act.dma_start(taps[j:P:J, :, J - 1 - j:J - 1 - j + TAPS],
                              conv_w.rearrange("o c k -> c o k")).then_inc(taps_in, 16)

            def xhi(b, c):
                if c == 0 and not isinstance(b, int):
                    act.wait_ge(conv_ready, b * CONVS)
                act.wait_ge(xt_done, b * CHUNKS + (c + 1))
                nc.scalar.activation(x_chunk(x_hi, c), x_turn(c), ACT.Copy).then_inc(xhi_done, 1)

            def yhi(b, i):
                act.wait_ge(y_turned, b * CONVS + (i + 1))
                nc.scalar.activation(y_part(y_hi, i // G, i % G), y_turn(i), ACT.Copy).then_inc(yhi_done, 1)

            def ahi(b):
                nc.scalar.activation(a_cur[:, :, 0, :].rearrange("p (a k) r -> p a k r", a=1),
                                     a_eff[:, bass.ds(b, 1), :, :], ACT.Copy).then_inc(ahi_done, 1)

            def ax_hi(b):
                act.wait_ge(ax_ready, b + 1)
                nc.scalar.activation(ax_sum[:, :], rank[R:2 * R, :], ACT.Copy).then_inc(ax_half, 1)
                act.wait_ge(ax_summed, b + 1)
                for q in (0, 2):
                    nc.scalar.activation(ax_st[q * R:(q + 1) * R, :], ax_sum[:, :], ACT.Copy).then_inc(axhi_done, 1)

            def whi(k):
                act.wait_ge(w_sum, k + 1)
                nc.scalar.activation(w_hi[:, k, :], w_raw[:, k, :], ACT.Copy).then_inc(whi_done, 1)

            for c in range(4):
                xhi(0, c)
            act.wait_ge(taps_in, 16 * J)
            for i in range(2 * J):
                nc.scalar.activation(toeplitz(t_hi, i), toeplitz_in(i), ACT.Copy).then_inc(thi_done, 1)
            for c in range(4, CHUNKS):
                xhi(0, c)
            act.wait_ge(as_in, 64)
            for jl in range(2):
                nc.scalar.activation(ordered(as_st[:, :], jl), natural(as_rep[:, :], jl), ACT.Copy).then_inc(as_hi, 1)
            act.wait_ge(bs_tr, 1)
            for h in range(2):
                nc.scalar.activation(bs_cols(bs_st[:, :], h), bs_turned(main[1][:, :], h), ACT.Copy).then_inc(bs_hi, 1)
            act.wait_ge(la_in, 16 * RQ)
            for jl in range(2):
                nc.scalar.activation(ordered(flat(la_ord[:, :, :]), jl), natural(flat(la[:, :, :]), jl),
                                     ACT.Copy).then_inc(la_ordered, 1)
            for i in range(CONVS):
                yhi(0, i)
            act.wait_ge(la_ordered, 2)
            act.wait_ge(lb_in, 16)
            nc.scalar.activation(lb_ord[:, :, :, :], lb[:, :, :, :].rearrange("p n j r -> p n (j r)")
                                 .rearrange("p n (x r) -> p x n r", r=R8), ACT.Copy).then_inc(lb_ordered, 1)
            act.wait_ge(ctx_done, 1)
            for k in range(KC):
                act.wait_ge(a_mm, (k | 1) + 1)
                nc.scalar.activation(a_eff[:, :, k, :].rearrange("p b (q r) -> p q b r", q=RQ),
                                     a_out(k).rearrange("p (q b r) -> p q b r", q=RQ, b=NB), ACT.Copy).then_inc(a_done, 1)
            for q in range(RQ):
                act.wait_ge(lb_tr, q + 1)
                nc.scalar.activation(lbt[:, q, :].rearrange("s (p j) -> s j p", j=J),
                                     main[q % 2][:, :].rearrange("s (j p) -> s j p", j=J), ACT.Copy).then_inc(lbt_done, 1)
            for k in range(4):
                whi(k)
            for i in range(2 * RQ):
                act.wait_ge(be_mm, i + 1)
                nc.scalar.activation(be[0:64, i // 2, (i % 2) * 512:(i % 2 + 1) * 512],
                                     conv[i % CBANKS][0:NB * R8, :], ACT.Copy).then_inc(be_hi, 1)
            act.wait_ge(a_done, KC)
            ahi(0)
            act.wait_ge(be_out, 16 * 2 * RQ)
            for k in range(4, KC):
                whi(k)
            ax_hi(0)

            with act.Fori(1, NB) as b:
                for c in range(CHUNKS):
                    xhi(b, c)
                act.wait_ge(ax_ready, b)
                ahi(b)
                act.wait_ge(tile_done, b * TT)
                for i in range(CONVS):
                    yhi(b, i)
                ax_hi(b)

        @block.vector
        def _(dve):
            dve.sem_inc(main_free, 2)
            dve.sem_inc(conv_free, CONVS)

            def xturn(b, c):
                if isinstance(b, int):
                    if c % 4 == 0:
                        dve.wait_ge(x_first[c // 4], 64)
                elif c == 0:
                    dve.wait_ge(x_loaded, b * 64)
                if c >= 2:
                    dve.wait_ge(xlo_done, b * CHUNKS + (c - 1))
                elif not isinstance(b, int):
                    dve.wait_ge(xlo_done, b * CHUNKS)
                m = XSTART[c + 1] - XSTART[c]
                blocks = x_in[:, :, :].rearrange("p c (m j) -> p m c j", j=J)[:, XSTART[c]:XSTART[c + 1]]
                nc.vector.transpose(x_stage[:, c % 2, 0:m * NG].rearrange("p (m s) -> p m s", s=NG),
                                    blocks).then_inc(xt_done, 1)

            def xlo(b, c):
                dve.wait_ge(xhi_done, b * CHUNKS + (c + 1))
                nc.vector.tensor_tensor(x_chunk(x_lo, c), x_turn(c), x_chunk(x_hi, c).bitcast(F32),
                                        ALU.subtract).then_inc(xlo_done, 1)

            def x_steps(b, c0, c1):
                for c in range(c0, c1):
                    xturn(b, c)
                    if c > c0:
                        xlo(b, c - 1)
                xlo(b, c1 - 1)

            def y_steps(b):
                def turn(i):
                    if i >= 2:
                        dve.wait_ge(ylo_done, b * CONVS + (i - 1))
                    elif not isinstance(b, int):
                        dve.wait_ge(ylo_done, b * CONVS + (i - 1))
                    dve.wait_ge(conv_free, b * CONVS + (i + 1 + CONVS))
                    src = y_add[:, i % 2, :].rearrange("p (a m n) -> p a n m", a=2, n=SB)
                    dst = y_stage[:, i % 2, :].rearrange("p (a q n) -> p a n q", a=2, n=SB)
                    nc.vector.transpose(dst, src).then_inc(y_turned, 1)

                for i in range(CONVS):
                    g = i % G
                    dve.wait_ge(conv_ready, b * CONVS + (i + 1))
                    if i >= 2:
                        dve.wait_ge(y_turned, b * CONVS + (i - 1))
                    elif not isinstance(b, int):
                        dve.wait_ge(y_turned, b * CONVS + (i - 1))
                    term = ctx_all[:, g, bass.ds(b * SB, SB)].unsqueeze(1).broadcast_to([P, 64, SB])
                    nc.vector.tensor_tensor(y_add[:, i % 2, :].rearrange("p (m n) -> p m n", n=SB),
                                            conv[i % CBANKS][:, :].rearrange("p (m n) -> p m n", n=SB),
                                            term, ALU.add).then_inc(conv_free, 1)
                    if i >= 1:
                        turn(i - 1)
                turn(CONVS - 1)

            def ax_steps(b):
                dve.wait_ge(ax_half, b + 1)
                nc.vector.tensor_tensor(ax_sum[:, :], rank[0:R, :], ax_sum[:, :], ALU.add).then_inc(ax_summed, 1)
                dve.wait_ge(axhi_done, b * 2 + 2)
                for q in (1, 3):
                    nc.vector.tensor_tensor(ax_st[q * R:(q + 1) * R, :], ax_sum[:, :],
                                            ax_st[0:R, :].bitcast(F32), ALU.subtract).then_inc(axlo_done, 1)

            def finish(b, cl):
                dve.wait_ge(tile_done, b * TT + (cl + 1))
                dve.wait_ge(res_ready, b * TT + (cl + 1))
                nc.vector.tensor_tensor(res[:, cl, :], main[cl % 2][:, :], res[:, cl, :],
                                        ALU.add).then_inc(main_free, 1)

            nc.vector.memset(taps[:, :, :], 0.0).then_inc(taps_zero, 1)
            dve.wait_ge(gate_in, 16)
            nc.vector.tensor_copy(gate_rep[:, :, :], gate_nat[:, :].unsqueeze(2).broadcast_to([NB, NL, R8])).then_inc(gate_cp, 1)
            dve.wait_ge(ctx_tr, 1)
            nc.vector.tensor_copy(cond_t[:, :], rank[:, 0:NS]).then_inc(ctx_cp, 1)
            for g in range(G):
                nc.vector.tensor_copy(
                    cw_rep[:, g, :].rearrange("p (j l h) -> p j l h", j=J, l=CL),
                    rank[:, NS + g * CG:NS + (g + 1) * CG].rearrange("p (h l) -> p l h", l=CL)
                    .unsqueeze(1).broadcast_to([P, J, CL, CH])).then_inc(ctx_cp, 1)
                nc.vector.tensor_copy(
                    bias_rep[:, g, :].rearrange("p (j l h) -> p j l h", j=J, l=CL),
                    bias_nat[:, g * CG:(g + 1) * CG].rearrange("p (h l) -> p l h", l=CL)
                    .unsqueeze(1).broadcast_to([1, J, CL, CH])).then_inc(ctx_cp, 1)
            dve.wait_ge(halo_zero, 2)
            for c in range(4):
                xturn(0, c)
            for i in range(2 * J):
                dve.wait_ge(thi_done, i + 1)
                nc.vector.tensor_tensor(toeplitz(t_lo, i), toeplitz_in(i), toeplitz(t_hi, i).bitcast(F32),
                                        ALU.subtract).then_inc(tlo_done, 1)
            for c in range(4, CHUNKS):
                xturn(0, c)
            dve.wait_ge(ctx_mm, 1)
            nc.vector.tensor_copy(ctx_all[:, :, :].rearrange("p g n -> p (g n)"), conv[0][:, 0:G * NS]).then_inc(ctx_done, 1)
            dve.wait_ge(bs_in, 16)
            nc.vector.tensor_copy(bs_rep[:, :, :, :], bs_nat[:, :, :].unsqueeze(2).broadcast_to([P, J, 4, R])).then_inc(bs_cp, 1)
            nc.vector.tensor_reduce(diag[:, :], ident[:, :].rearrange("p (n r) -> p r n", r=R8), AX.X, ALU.add).then_inc(diag_done, 1)
            dve.wait_ge(diag_done, 1)
            nc.vector.tensor_tensor(gmix[:, :, :], diag[:, :].unsqueeze(1).broadcast_to([P, NB, R8]),
                                    rank[:, P:P + NB].unsqueeze(2).broadcast_to([P, NB, R8]), ALU.mult).then_inc(gmix_done, 1)
            y_steps(0)
            for jl in range(2):
                dve.wait_ge(as_hi, jl + 1)
                nc.vector.tensor_tensor(ordered(as_st[64:P, :], jl), natural(as_rep[64:P, :], jl),
                                        ordered(as_st[64:P, :], jl).bitcast(F32), ALU.subtract).then_inc(as_lo, 1)
            dve.wait_ge(bs_hi, 2)
            for h in range(2):
                for q in (1, 3):
                    rows = slice(q * R, (q + 1) * R)
                    nc.vector.tensor_tensor(bs_cols(bs_st[rows, :], h), bs_turned(main[1][rows, :], h),
                                            bs_cols(bs_st[rows, :], h).bitcast(F32), ALU.subtract).then_inc(bs_lo, 1)
            for k in range(KC):
                dve.wait_ge(kern_in[k // 4], 64)
                dve.wait_ge(w_mm, k + 1)
                nc.vector.tensor_tensor(w_raw[:, k, :], main[k % 2][:, :], w_raw[:, k, :], ALU.add).then_inc(w_sum, 1)

            def w_lo_odd(k):
                dve.wait_ge(whi_done, k + 1)
                nc.vector.tensor_tensor(w_lo[:, k, :], w_raw[:, k, :], w_hi[:, k, :].bitcast(F32),
                                        ALU.subtract).then_inc(wlo_done[1], 1)

            w_lo_odd(1)
            w_lo_odd(3)
            for i in range(2 * RQ):
                dve.wait_ge(be_hi, i + 1)
                half = slice((i % 2) * 512, (i % 2 + 1) * 512)
                nc.vector.tensor_tensor(be[64:P, i // 2, half], conv[i % CBANKS][0:NB * R8, :],
                                        be[0:64, i // 2, half].bitcast(F32), ALU.subtract).then_inc(be_lo, 1)
            w_lo_odd(5)
            w_lo_odd(7)
            ax_steps(0)
            with dve.Fori(1, NB) as b:
                finish(b - 1, 0)
                x_steps(b, 0, 3)
                finish(b - 1, 1)
                x_steps(b, 3, 6)
                finish(b - 1, 2)
                x_steps(b, 6, CHUNKS)
                finish(b - 1, 3)
                y_steps(b)
                ax_steps(b)
            for cl in range(TT):
                finish(NB - 1, cl)

        @block.tensor
        def _(pe):
            mm = nc.tensor.matmul

            pe.wait_ge(ident_ready, 2)
            pe.wait_ge(ctx_in, 48)
            pe.wait_ge(gate_cp, 1)
            mm(rank[:, P:P + NB], gate_rep[:, :, :].rearrange("b n r -> b (n r)"), ident[0:NB, 0:NB],
               start=True, stop=True)
            nc.tensor.transpose(rank[:, 0:NS], cond_nat[:, :], ident[0:NS, 0:NS])
            nc.tensor.transpose(rank[:, NS:NS + C], cw_nat[:, :], ident[0:C, 0:C]).then_inc(ctx_tr, 1)
            pe.wait_ge(ctx_cp, 1 + 2 * G)
            pe.wait_ge(ones_done, 1)
            for g in range(G):
                mm(conv[0][:, g * NS:(g + 1) * NS], cw_rep[:, g, :], cond_t[:, :], start=True, stop=False)
                last = mm(conv[0][:, g * NS:(g + 1) * NS], bias_rep[:, g, :], ones[:, :], start=False, stop=True)
            last.then_inc(ctx_mm, 1)
            pe.wait_ge(bs_cp, 1)
            for j in range(J):
                last = nc.tensor.transpose(main[1][:, j * P:(j + 1) * P],
                                           bs_rep[:, j, :, :].rearrange("p a r -> p (a r)"), ident[:, :])
            last.then_inc(bs_tr, 1)

            def convolve(b):
                pe.wait_ge(xlo_done, b * CHUNKS + CHUNKS)
                for i in range(CONVS):
                    mh, g = i // G, i % G
                    before = i - CBANKS if i >= CBANKS else (6, 7, 5)[i] - CONVS
                    pe.wait_ge(conv_free, b * CONVS + (before + 1 + CONVS))
                    n = 0
                    for w in range(2):
                        rows = slice(mh * 64 + w, mh * 64 + w + 64)
                        for lhs, rhs in ((t_hi, x_hi), (t_hi, x_lo), (t_lo, x_hi)):
                            last = mm(conv[i % CBANKS][:, :], lhs[:, w, g, :],
                                      rhs[:, g, rows, :].rearrange("p m n -> p (m n)"), start=n == 0, stop=n == 5)
                            n += 1
                    last.then_inc(conv_ready, 1)

            pe.wait_ge(tlo_done, 2 * J)
            pe.wait_ge(ctx_done, 1)
            convolve(0)
            pe.wait_ge(la_ordered, 2)
            pe.wait_ge(gmix_done, 1)
            pe.wait_ge(bs_lo, 4)
            for k in range(KC):
                for q in range(RQ):
                    last = mm(a_out(k)[:, q * 64:(q + 1) * 64], la_ord[:, q, k * P:(k + 1) * P],
                              gmix[:, :, :].rearrange("p b r -> p (b r)"), start=True, stop=True)
                last.then_inc(a_mm, 1)
            pe.wait_ge(lb_ordered, 1)
            for q in range(RQ):
                if q < 2:
                    pe.wait_ge(a_done, 4 * q + 4)
                else:
                    pe.wait_ge(lbt_done, q - 1)
                for j in range(J):
                    t = nc.tensor.transpose(main[q % 2][:, j * P:(j + 1) * P],
                                            lb_ord[:, j * RQ + q, :, :].rearrange("p n r -> p (n r)"), ident[:, :])
                t.then_inc(lb_tr, 1)
            pe.wait_ge(as_lo, 2)
            for k in range(KC):
                if k < 2:
                    pe.wait_ge(lbt_done, k + 3)
                else:
                    pe.wait_ge(w_sum, k - 1)
                for h in range(2):
                    last = mm(main[k % 2][:, h * 512:(h + 1) * 512], as_st[:, k * P:(k + 1) * P],
                              bs_st[:, h * 512:(h + 1) * 512], start=True, stop=True)
                last.then_inc(w_mm, 1)
            for i in range(2 * RQ):
                q, h = i // 2, i % 2
                if i < CBANKS:
                    pe.wait_ge(conv_free, 2 * CONVS)
                else:
                    pe.wait_ge(be_lo, i - CBANKS + 1)
                mm(conv[i % CBANKS][0:NB * R8, :], gmix[:, :, :].rearrange("p b r -> p (b r)"),
                   lbt[:, q, h * 512:(h + 1) * 512], start=True, stop=True).then_inc(be_mm, 1)

            def dense(b, cl, k):
                yh = y_hi[:, (k * CL + cl) * CH:(k * CL + cl + 1) * CH, :].rearrange("p h s -> p (h s)")
                yl = y_lo[:, (k * CL + cl) * CH:(k * CL + cl + 1) * CH, :].rearrange("p h s -> p (h s)")
                for lhs, rhs, first in ((yh, w_hi, True), (yh, w_lo, False), (yl, w_hi, False)):
                    for h in range(2):
                        mm(main[cl % 2][:, h * 512:(h + 1) * 512], lhs, rhs[:, k, h * 512:(h + 1) * 512],
                           start=k == 0 and first, stop=False)

            def tokens(b):
                for cl in range(TT):
                    pe.wait_ge(main_free, b * TT + (cl + 1))
                    for k in range(KC):
                        if cl == 0:
                            pe.wait_ge(wlo_done[k % 2], k // 2 + 1)
                        if cl == 0 and k == 0:
                            pe.wait_ge(ylo_done, b * CONVS + G)
                        if cl == 0 and k == 4:
                            pe.wait_ge(ylo_done, b * CONVS + CONVS)
                            pe.wait_ge(acur_done, b + 1)
                            for kk in range(KC):
                                lhs = a_cur[:, kk, :, :].rearrange("p a r -> p (a r)")
                                for y in (y_hi, y_lo):
                                    last = mm(rank[0:2 * R, :], lhs,
                                              y[:, kk * 16:(kk + 1) * 16, :].rearrange("p q s -> p (q s)"),
                                              start=kk == 0 and y is y_hi, stop=kk == KC - 1 and y is y_lo)
                            last.then_inc(ax_ready, 1)
                        dense(b, cl, k)
                    if cl == 0:
                        pe.wait_ge(axlo_done, b * 2 + 2)
                        pe.wait_ge(b_loaded, b * 64 + 64)
                    for h in range(2):
                        last = mm(main[cl % 2][:, h * 512:(h + 1) * 512], ax_st[:, cl * P:(cl + 1) * P],
                                  b_cur[:, h * 512:(h + 1) * 512], start=False, stop=True)
                    last.then_inc(tile_done, 1)

            pe.wait_ge(w_sum, KC)
            with pe.Fori(0, NB - 1) as b:
                tokens(b)
                convolve(b + 1)
            tokens(NB - 1)


_INS = ['x', 'cond_128', 'fside_S_0', 'L0_cond_weight', 'L0_cond_c_weight', 'L0_ffn_gate', 'L0_ffn_kernel',
        'L0_ffn_bias', 'L0_ffn_lora_A', 'L0_ffn_lora_B', 'L0_ffn_lora_A_shared', 'L0_ffn_lora_B_shared']


def kernel(**inputs):
    import concourse.bacc as bacc
    from concourse.bass_utils import run_bass_kernel_spmd

    nc = bacc.Bacc("TRN2", target_bir_lowering=False, num_devices=1)
    arrays, args = {}, []
    for name in _INS:
        a = np.ascontiguousarray(inputs[name])
        arrays[f"in_{name}"] = a
        args.append(nc.dram_tensor(f"in_{name}", a.shape, mybir.dt.from_np(a.dtype), kind="ExternalInput").ap())
    args.append(nc.dram_tensor("out", (NS, C, L), F32, kind="ExternalOutput").ap())
    adaln_ffn(nc, *args)
    r = run_bass_kernel_spmd(nc, [arrays], core_ids=[0])
    return r.results[0]["out"]
```

```python
import numpy as np
import concourse.bass as bass
from concourse import mybir
from contextlib import ExitStack

F32 = mybir.dt.float32
F32R = mybir.dt.float32r
ALU = mybir.AluOpType
ACT = mybir.ActivationFunctionType
AX = mybir.AxisListType

P = 128
NS, C, L = 64, 64, 1024
D = 1024
G, CG, TAPS = 4, 16, 9
CD = 128
NL, R = 16, 32
NB = 8
SB = NS // NB
J = 8
CL, CH = 4, 4
M = L // J
MB = M + 1
HALO = TAPS // 2
KC = 8
TT = SB * C // P
NG = SB * G
CHUNKS = 8
XSTART = [0, 16, 32, 48, 65, 81, 97, 113, MB]
XHALF = 528
XSTAGE = 17 * NG
CONVS = 2 * G
CBANKS = 3
R8 = 8
RQ = R // R8
STACK = 3 * R
DVE_W = (5, 7)
POOL_T = 10
POOL_X = (1, 5, 7)


def adaln_ffn(nc, x, cond, cond_bias, conv_w, cond_w, gate, kern, bias,
              lora_a, lora_b, lora_as, lora_bs, out):
    b_scratch = nc.dram_tensor("b_scratch", [2, NB, R, D], F32, kind="Internal").ap()

    x_v = x.rearrange("n (g ch cl) l -> (n g) ch cl l", g=G, ch=CH)
    out_v = out.rearrange("n (g ch cl) l -> (n g) ch cl l", g=G, ch=CH)
    kern_v = kern.rearrange("(ma mm jh jl) d -> ma jh mm (jl d)", ma=4, mm=32, jh=4)
    la_v = lora_a.rearrange("n (r q) l -> (n r) q l", q=RQ)

    ctx = ExitStack()
    with ctx:
        def sb(name, shape, dt=F32):
            return ctx.enter_context(nc.sbuf_tensor(name, shape, dt))

        def ps(name, shape):
            return ctx.enter_context(nc.psum_tensor(name, shape, F32))

        def sem(name):
            return ctx.enter_context(nc.semaphore(name))

        def early(*specs):
            with ExitStack() as own:
                return [own.enter_context(nc.sbuf_tensor(*s)) for s in specs]

        la, lb = early(("la", [P, RQ, L], F32), ("lb", [P, NL, J, R], F32))
        lb_ord, be = early(("lb_ord", [P, J * RQ, NL, R8], F32), ("be", [P, RQ, D], F32R))
        w_hi = sb("w_hi", [P, KC, D], F32R)
        bs_rep, = early(("bs_rep", [P, J, 3, R], F32))
        w_raw, = early(("w_raw", [P, KC, D], F32))
        w_lo = sb("w_lo", [P, KC, D], F32R)
        y_hi = sb("y_hi", [P, KC * CL * CH, NG], F32R)
        y_lo = sb("y_lo", [P, KC * CL * CH, NG], F32R)
        x_hi = sb("x_hi", [P, G, MB, SB], F32R)
        x_lo = sb("x_lo", [P, G, MB, SB], F32R)
        x_in = sb("x_in", [P, CL, L + 2 * HALO])
        la_ord, = early(("la_ord", [P, KC, RQ, P], F32))
        lbt, = early(("lbt", [P, RQ, D], F32))
        res = sb("res", [P, CL, D])
        t_hi = sb("t_hi", [P, 2, G, P], F32R)
        t_lo = sb("t_lo", [P, 2, G, P], F32R)
        x_stage = sb("x_stage", [P, 2, XSTAGE])
        cond_nat, cw_nat, cond_t, cw_rep = early(
            ("cond_nat", [NS, CD], F32), ("cw_nat", [C, CD], F32), ("cond_t", [CD, NS], F32),
            ("cw_rep", [P, G, P], F32))
        y_add = sb("y_add", [P, 2, 512])
        y_stage = sb("y_stage", [P, 2, 512])
        as_st, = early(("as_st", [P, L], F32R))
        bias_all = sb("bias_all", [P, D])
        a_eff = sb("a_eff", [P, NB, KC, R])
        taps, = early(("taps", [P, C, 2 * J], F32))
        b_cur = sb("b_cur", [P, D], F32R)
        as_rep, = early(("as_rep", [P, L], F32))
        ax_st = sb("ax_st", [P, 512], F32R)
        ax_sum = sb("ax_sum", [R, 512])
        bs_st, = early(("bs_st", [P, D], F32R))
        a_cur = sb("a_cur", [P, KC, 2, R], F32R)
        bs_nat = sb("bs_nat", [P, J, R])
        sb("bs_st_rest", [P, 256])
        ctx_all = sb("ctx_all", [P, G, NS])
        ident = sb("ident", [P, P])
        gate_nat = sb("gate_nat", [NB, NL])
        gate_rep = sb("gate_rep", [NB, NL, R8])
        diag = sb("diag", [P, R8])
        gmix = sb("gmix", [P, NB, R8])
        bias_nat = sb("bias_nat", [G, CG])
        bias_col = sb("bias_col", [P, G])
        bias_rep = sb("bias_rep", [G, P])

        main = [ps(f"main{i}", [P, D]) for i in range(2)]
        conv = [ps(f"conv{i}", [P, 512]) for i in range(CBANKS)]
        rank = ps("rank", [P, 512])

        taps_zero, halo_zero, ident_ready = sem("taps_zero"), sem("halo_zero"), sem("ident_ready")
        taps_in, ctx_in, bs_in, as_in = sem("taps_in"), sem("ctx_in"), sem("bs_in"), sem("as_in")
        gate_cp = sem("gate_cp")
        gate_in, la_in = sem("gate_in"), [sem(f"la_in{ma}") for ma in range(4)]
        lb_in = [sem(f"lb_in{h}") for h in range(2)]
        kern_in = [sem(f"kern_in{ma}") for ma in range(4)]
        bias_in, cbias_in = sem("bias_in"), sem("cbias_in")
        thi_done, tlo_done, tlo_pool = sem("thi_done"), sem("tlo_done"), sem("tlo_pool")
        gate_tr, bias_rep_done, bcol_done = sem("gate_tr"), sem("bias_rep_done"), sem("bcol_done")
        ctx_tr, ctx_cp, ctx_mm, ctx_done = sem("ctx_tr"), sem("ctx_cp"), sem("ctx_mm"), sem("ctx_done")
        bs_cp, bs_tr, bs_hi, bs_lo = sem("bs_cp"), sem("bs_tr"), sem("bs_hi"), sem("bs_lo")
        as_hi, as_lo = sem("as_hi"), sem("as_lo")
        w_mm, w_sum, whi_done, wlo_done = sem("w_mm"), sem("w_sum"), sem("whi_done"), sem("wlo_done")
        wlo_own = sem("wlo_own")
        diag_done, gmix_done = sem("diag_done"), sem("gmix_done")
        la_ordered, lb_ordered = sem("la_ordered"), sem("lb_ordered")
        a_mm, a_done = sem("a_mm"), sem("a_done")
        lb_tr, lbt_done, be_mm = sem("lb_tr"), sem("lbt_done"), sem("be_mm")
        be_hi, be_lo, be_out = sem("be_hi"), sem("be_lo"), sem("be_out")
        x_first = [sem(f"x_first{i}") for i in range(2)]
        x_loaded, xt_done, xhi_done, xlo_done = sem("x_loaded"), sem("xt_done"), sem("xhi_done"), sem("xlo_done")
        xlo_pool = sem("xlo_pool")
        conv_ready, conv_free, y_turned = sem("conv_ready"), sem("conv_free"), sem("y_turned")
        yhi_done, ylo_done = sem("yhi_done"), sem("ylo_done")
        ylo_own = sem("ylo_own")
        ahi_done, acur_done, b_loaded = sem("ahi_done"), sem("acur_done"), sem("b_loaded")
        ax_ready, ax_half, ax_summed = sem("ax_ready"), sem("ax_half"), sem("ax_summed")
        axhi_done, axlo_done = sem("axhi_done"), sem("axlo_done")
        tile_done, main_free = sem("tile_done"), sem("main_free")
        res_ready = sem("res_ready")
        stored = [sem(f"stored{c}") for c in range(TT)]

        block = ctx.enter_context(nc.Block())

        def y_part(y, mh, g):
            return y[:, mh * 64:(mh + 1) * 64, :].rearrange("p q (n g) -> p q n g", g=G)[:, :, :, g]

        def y_turn(i):
            return y_stage[:, i % 2, :].rearrange("p (q n) -> p q n", n=SB)

        def x_chunk(t, c):
            m0, m1 = XSTART[c], XSTART[c + 1]
            return t[:, :, m0:m1, :].rearrange("p g m n -> p m g n")

        def x_turn(c):
            m = XSTART[c + 1] - XSTART[c]
            return x_stage[:, c % 2, 0:m * NG].rearrange("p (m n g) -> p m g n", n=SB, g=G)

        def toeplitz(t, i):
            at = (J - 1 - i % J) * CG
            return t[:, i // J, :, at:at + CG].rearrange("p g (l h) -> p g l h", h=CH)

        def toeplitz_in(i):
            return taps[:, :, i].rearrange("p (g h l) -> p g l h", g=G, h=CH)

        def bs_cols(t, h):
            return t.rearrange("q (p j) -> q j p", j=J)[:, 4 * h:4 * h + 4, :]

        def bs_turned(t):
            return t.rearrange("q (j p) -> q j p", j=4)

        def a_out(k):
            return main[k // 4][:, (k % 4) * 256:(k % 4 + 1) * 256]

        def la_chunk(k):
            return (la[:, :, (k // 2) * 256:(k // 2 + 1) * 256]
                    .rearrange("p q (m h l) -> p q h m l", h=4, l=2)[:, :, :, :, k % 2])

        def la_turned(t, k):
            return t[:, k, :, :].rearrange("p q (h m) -> p q h m", h=4)

        def ordered(t, jl):
            return t.rearrange("p (q l h m) -> p q l h m", l=2, h=4, m=32)[:, :, jl]

        def natural(t, jl):
            return t.rearrange("p (q m h l) -> p q h m l", m=32, h=4, l=2)[:, :, :, :, jl]

        def lb_part(n4):
            ns = slice(4 * n4, 4 * n4 + 4)
            return (lb_ord[:, :, ns, :].rearrange("p (j q) n r -> p n j q r", q=RQ),
                    lb[:, ns, :, :].rearrange("p n j (r q) -> p n j q r", q=RQ))

        def w_bank(m):
            if m < 4:
                return main[m // 2][:, (m % 2) * 512:(m % 2 + 1) * 512]
            return (rank, *conv)[m % 4][:, :]

        def y_split(b, i):
            if i % G == 3:
                return ylo_own, b * 2 + (i // G + 1)
            return ylo_done, b * (CONVS - 2) + (i + 1 - i // G)

        def w_split(k):
            own = sum(1 for i in DVE_W if i <= k)
            return (wlo_own, own) if k in DVE_W else (wlo_done, k + 1 - own)

        def x_split(b, c):
            if not isinstance(b, int):
                return xlo_done, (b - 1) * CHUNKS + (c + 1 + CHUNKS - len(POOL_X))
            if c in POOL_X:
                return xlo_pool, sum(1 for i in POOL_X if i <= c)
            return xlo_done, c + 1 - sum(1 for i in POOL_X if i <= c)

        @block.sync
        def _(sp):
            sp.dma_start(gate_nat[:, :], gate).then_inc(gate_in, 16)
            for ma in range(4):
                cols = slice(ma * 256, (ma + 1) * 256)
                sp.dma_start(la[:, :, cols], la_v[:, :, cols]).then_inc(la_in[ma], 16)
                if ma == 1:
                    sp.dma_start(cond_nat[:, :], cond).then_inc(ctx_in, 16)
                    sp.dma_start(cw_nat[:, :], cond_w).then_inc(ctx_in, 16)
                    sp.dma_start(bs_nat[:, :, :], lora_bs.rearrange("(p j) r -> p j r", j=J)).then_inc(bs_in, 16)
                    sp.dma_start(bias_nat[:, :], cond_bias.rearrange("(g c) -> g c", g=G)).then_inc(cbias_in, 16)

            def load_x(b):
                for ch in range(CH):
                    sp.dma_start(x_in[ch * NG:(ch + 1) * NG, :, HALO:HALO + L],
                                 x_v[bass.ds(b * NG, NG), ch, :, :]).then_inc(x_loaded, 16)

            def load_first(half):
                at, end = ((0, XHALF), (XHALF, L))[half]
                for ch in range(CH):
                    sp.dma_start(x_in[ch * NG:(ch + 1) * NG, :, HALO + at:HALO + end],
                                 x_v[0:NG, ch, :, at:end]).then_inc(x_first[half], 16)

            load_first(0)
            sp.wait_ge(taps_zero, 1)
            for j in range(J):
                sp.dma_start(taps[j:P:J, :, J - 1 - j:J - 1 - j + TAPS],
                             conv_w.rearrange("o c k -> c o k")).then_inc(taps_in, 16)
            load_first(1)
            for h in range(2):
                ns = slice(8 * h, 8 * h + 8)
                sp.dma_start(lb[:, ns, :, :].rearrange("p n j r -> p n (j r)"),
                             lora_b[ns].rearrange("n (p j) r -> p n (j r)", j=J)).then_inc(lb_in[h], 16)
            for q in range(3):
                sp.dma_start(as_rep[q * R:(q + 1) * R, :], lora_as).then_inc(as_in, 16)
            sp.wait_ge(bs_tr, 1)
            for ma in range(4):
                for jh in range(4):
                    sp.dma_start(w_raw[jh * 32:(jh + 1) * 32, 2 * ma:2 * ma + 2, :].rearrange("m j d -> m (j d)"),
                                 kern_v[ma, jh]).then_inc(kern_in[ma], 16)
            for q in range(RQ):
                sp.wait_ge(be_hi, 2 * q + 2)
                sp.wait_ge(be_lo, 2 * q + 2)
                for h in range(2):
                    sp.dma_start(b_scratch[h].rearrange("b (r q) d -> (b r) q d", q=RQ)[:, q, :],
                                 be[h * 64:(h + 1) * 64, q, :].bitcast(F32)).then_inc(be_out, 16)
            sp.wait_ge(w_mm, 2 * KC)
            sp.dma_start(bias_all[:, :], bias.partition_broadcast(P)).then_inc(bias_in, 16)
            sp.wait_ge(be_out, 16 * 2 * RQ)

            def load_b(b):
                for q, part in enumerate((0, 1, 0)):
                    sp.dma_start(b_cur[q * R:(q + 1) * R, :].bitcast(F32).rearrange("r (a d) -> r a d", a=1),
                                 b_scratch[part, bass.ds(b, 1), :, :].rearrange("a r d -> r a d")).then_inc(b_loaded, 16)

            def store(b, tiles=TT):
                for cl in range(tiles):
                    sp.wait_ge(main_free, b * TT + (cl + 3))
                    for ch in range(CH):
                        sp.dma_start(out_v[bass.ds(b * NG, NG), ch, cl, :],
                                     res[ch * NG:(ch + 1) * NG, cl, :]).then_inc(stored[cl], 16)

            sp.wait_ge(tlo_pool, POOL_T)
            sp.wait_ge(tlo_done, 2 * J - POOL_T)
            load_b(0)
            sp.wait_ge(res_ready, TT)
            sp.wait_ge(xt_done, CHUNKS)
            load_x(1)
            store(0)
            with sp.Fori(1, NB - 1) as b:
                sp.wait_ge(tile_done, b * TT)
                load_b(b)
                sp.wait_ge(res_ready, b * TT + TT)
                sp.wait_ge(xt_done, b * CHUNKS + CHUNKS)
                load_x(b + 1)
                store(b)
            sp.wait_ge(tile_done, (NB - 1) * TT)
            load_b(NB - 1)
            store(NB - 1, TT - 1)
            for h in range(2):
                sp.wait_ge(main_free, NB * TT + 2 + h)
                half = slice(h * 512, (h + 1) * 512)
                for ch in range(CH):
                    sp.dma_start(out_v[(NB - 1) * NG:NB * NG, ch, TT - 1, half],
                                 res[ch * NG:(ch + 1) * NG, TT - 1, half]).then_inc(stored[TT - 1], 16)
            for cl in range(TT):
                sp.wait_ge(stored[cl], 16 * CH * (NB + (cl == TT - 1)))

        @block.gpsimd
        def _(pool):
            nc.gpsimd.memset(ident[:, :], 0.0).then_inc(ident_ready, 1)
            nc.gpsimd.memset(x_in[:, :, 0:HALO], 0.0).then_inc(halo_zero, 1)
            nc.gpsimd.memset(x_in[:, :, HALO + L:], 0.0).then_inc(halo_zero, 1)
            pool.wait_ge(ident_ready, 1)
            nc.gpsimd.affine_select(out=ident[:, :], in_=ident[:, :], compare_op=ALU.not_equal, fill=1.0,
                                    base=0, pattern=[[-1, P]], channel_multiplier=1).then_inc(ident_ready, 1)
            pool.wait_ge(bs_in, 16)
            nc.gpsimd.tensor_copy(bs_rep[:, :, :, :], bs_nat[:, :, :].unsqueeze(2).broadcast_to([P, J, 3, R])).then_inc(bs_cp, 1)
            for c in POOL_X:
                pool.wait_ge(xhi_done, c + 1)
                nc.gpsimd.tensor_tensor(x_chunk(x_lo, c), x_turn(c), x_chunk(x_hi, c).bitcast(F32),
                                        ALU.subtract).then_inc(xlo_pool, 1)
                if c == POOL_X[0]:
                    for i in range(POOL_T):
                        pool.wait_ge(thi_done, i + 1)
                        nc.gpsimd.tensor_tensor(toeplitz(t_lo, i), toeplitz_in(i), toeplitz(t_hi, i).bitcast(F32),
                                                ALU.subtract).then_inc(tlo_pool, 1)

            def a_lo(b):
                pool.wait_ge(ahi_done, b + 1)
                nc.gpsimd.tensor_tensor(
                    a_cur[:, :, 1, :].rearrange("p (a k) r -> p a k r", a=1),
                    a_eff[:, bass.ds(b, 1), :, :],
                    a_cur[:, :, 0, :].bitcast(F32).rearrange("p (a k) r -> p a k r", a=1),
                    ALU.subtract).then_inc(acur_done, 1)

            def y_los(b):
                for i in range(CONVS):
                    mh, g = i // G, i % G
                    if g == 3:
                        continue
                    pool.wait_ge(yhi_done, b * CONVS + (i + 1))
                    nc.gpsimd.tensor_tensor(y_part(y_lo, mh, g), y_turn(i),
                                            y_part(y_hi, mh, g).bitcast(F32), ALU.subtract).then_inc(ylo_done, 1)

            def residual(cl):
                nc.gpsimd.tensor_tensor(res[:, cl, :], x_in[:, cl, HALO:HALO + L], bias_all[:, :],
                                        ALU.add).then_inc(res_ready, 1)

            y_los(0)
            for k in range(KC):
                if k in DVE_W:
                    continue
                pool.wait_ge(whi_done, k + 1)
                nc.gpsimd.tensor_tensor(w_lo[:, k, :], w_raw[:, k, :], w_hi[:, k, :].bitcast(F32),
                                        ALU.subtract).then_inc(wlo_done, 1)
                if k == 4:
                    a_lo(0)
            pool.wait_ge(bias_in, 16)
            pool.wait_ge(be_mm, 2 * RQ)
            for cl in range(TT):
                residual(cl)
            with pool.Fori(1, NB) as b:
                a_lo(b)
                y_los(b)
                pool.wait_ge(x_loaded, b * 64)
                for cl in range(TT):
                    pool.wait_ge(stored[cl], b * 64)
                    residual(cl)

        @block.scalar
        def _(act):
            def xhi(b, c):
                if c == 0 and not isinstance(b, int):
                    act.wait_ge(conv_ready, b * CONVS)
                act.wait_ge(xt_done, b * CHUNKS + (c + 1))
                nc.scalar.activation(x_chunk(x_hi, c), x_turn(c), ACT.Copy).then_inc(xhi_done, 1)

            def yhi(b, i):
                act.wait_ge(y_turned, b * CONVS + (i + 1))
                nc.scalar.activation(y_part(y_hi, i // G, i % G), y_turn(i), ACT.Copy).then_inc(yhi_done, 1)

            def ahi(b):
                nc.scalar.activation(a_cur[:, :, 0, :].rearrange("p (a k) r -> p a k r", a=1),
                                     a_eff[:, bass.ds(b, 1), :, :], ACT.Copy).then_inc(ahi_done, 1)

            def ax_hi(b):
                act.wait_ge(ax_ready, b + 1)
                nc.scalar.activation(ax_sum[:, :], rank[R:2 * R, :], ACT.Copy).then_inc(ax_half, 1)
                act.wait_ge(ax_summed, b + 1)
                for q in range(2):
                    nc.scalar.activation(ax_st[q * R:(q + 1) * R, :], ax_sum[:, :], ACT.Copy).then_inc(axhi_done, 1)

            def whi(k):
                act.wait_ge(w_sum, 2 * k + 2)
                nc.scalar.activation(w_hi[:, k, :], w_raw[:, k, :], ACT.Copy).then_inc(whi_done, 1)

            for k in range(KC):
                if k % 2 == 0:
                    act.wait_ge(la_in[k // 2], 16)
                nc.scalar.activation(la_turned(la_ord, k), la_chunk(k), ACT.Copy).then_inc(la_ordered, 1)
            act.wait_ge(bs_tr, 1)
            for h in range(2):
                nc.scalar.activation(bs_cols(bs_st[0:STACK, :], h), bs_turned(conv[1 + h][0:STACK, :]),
                                     ACT.Copy).then_inc(bs_hi, 1)

            def t_his(i0, i1):
                for i in range(i0, i1):
                    nc.scalar.activation(toeplitz(t_hi, i), toeplitz_in(i), ACT.Copy).then_inc(thi_done, 1)

            def a_copies(k0, k1):
                for k in range(k0, k1):
                    act.wait_ge(a_mm, (k | 1) + 1)
                    nc.scalar.activation(a_eff[:, :, k, :].rearrange("p b (r q) -> p q b r", q=RQ),
                                         a_out(k).rearrange("p (q b r) -> p q b r", q=RQ, b=NB), ACT.Copy).then_inc(a_done, 1)

            def lb_part_copy(i):
                act.wait_ge(lb_in[i // 2], 16)
                dst, src = lb_part(i)
                nc.scalar.activation(dst, src, ACT.Copy).then_inc(lb_ordered, 1)

            for c in range(3):
                xhi(0, c)
            act.wait_ge(taps_in, 16 * J)
            t_his(0, J)
            xhi(0, 3)
            t_his(J, 2 * J)
            xhi(0, 4)
            xhi(0, 5)
            xhi(0, 6)
            lb_part_copy(0)
            xhi(0, 7)
            a_copies(0, 4)
            yhi(0, 0)
            lb_part_copy(1)
            yhi(0, 1)
            a_copies(4, KC)
            yhi(0, 2)
            lb_part_copy(2)
            yhi(0, 3)
            lb_part_copy(3)
            act.wait_ge(as_in, 48)
            for jl in range(2):
                nc.scalar.activation(ordered(as_st[0:STACK, :], jl), natural(as_rep[0:STACK, :], jl),
                                     ACT.Copy).then_inc(as_hi, 1)
            yhi(0, 4)

            def lb_copy(q):
                act.wait_ge(lb_tr, q + 1)
                nc.scalar.activation(lbt[:, q, :].rearrange("s (p j) -> s j p", j=J),
                                     main[q % 2][:, :].rearrange("s (j p) -> s j p", j=J), ACT.Copy).then_inc(lbt_done, 1)

            def be_his(i0, i1):
                for i in range(i0, i1):
                    act.wait_ge(be_mm, i + 1)
                    nc.scalar.activation(be[0:64, i // 2, (i % 2) * 512:(i % 2 + 1) * 512],
                                         conv[i % CBANKS][0:NB * R8, :], ACT.Copy).then_inc(be_hi, 1)

            lb_copy(0)
            yhi(0, 5)
            lb_copy(1)
            yhi(0, 6)
            be_his(0, 1)
            lb_copy(2)
            yhi(0, 7)
            be_his(1, 2)
            lb_copy(3)
            be_his(2, 5)
            whi(0)
            be_his(5, 8)
            whi(1)
            whi(2)
            whi(3)
            act.wait_ge(be_out, 16 * 2 * RQ)
            whi(4)
            whi(5)
            act.wait_ge(w_mm, 2 * KC)
            act.wait_ge(a_done, KC)
            ahi(0)
            whi(6)
            whi(7)
            ax_hi(0)

            with act.Fori(1, NB) as b:
                for c in range(CHUNKS):
                    xhi(b, c)
                act.wait_ge(ax_ready, b)
                ahi(b)
                act.wait_ge(tile_done, b * TT)
                for i in range(CONVS):
                    yhi(b, i)
                ax_hi(b)

        @block.vector
        def _(dve):
            dve.sem_inc(main_free, 2)
            dve.sem_inc(conv_free, CONVS)

            def xturn(b, c):
                if isinstance(b, int):
                    if c % 4 == 0:
                        dve.wait_ge(x_first[c // 4], 64)
                elif c == 0:
                    dve.wait_ge(x_loaded, b * 64)
                if c >= 2 or not isinstance(b, int):
                    dve.wait_ge(*x_split(b, c - 2))
                m = XSTART[c + 1] - XSTART[c]
                blocks = x_in[:, :, :].rearrange("p c (m j) -> p m c j", j=J)[:, XSTART[c]:XSTART[c + 1]]
                nc.vector.transpose(x_stage[:, c % 2, 0:m * NG].rearrange("p (m s) -> p m s", s=NG),
                                    blocks).then_inc(xt_done, 1)

            def xlo(b, c):
                dve.wait_ge(xhi_done, b * CHUNKS + (c + 1))
                nc.vector.tensor_tensor(x_chunk(x_lo, c), x_turn(c), x_chunk(x_hi, c).bitcast(F32),
                                        ALU.subtract).then_inc(xlo_done, 1)

            def x_steps(b, c0, c1):
                for c in range(c0, c1):
                    xturn(b, c)
                    if c > c0:
                        xlo(b, c - 1)
                xlo(b, c1 - 1)

            def y_turned_over(b, i):
                if i >= 2 or not isinstance(b, int):
                    dve.wait_ge(*(y_split(b, i - 2) if i >= 2 else y_split(b - 1, i - 2 + CONVS)))
                dve.wait_ge(conv_free, b * CONVS + (i + 1 + CONVS))
                src = y_add[:, i % 2, :].rearrange("p (a m n) -> p a n m", a=2, n=SB)
                dst = y_stage[:, i % 2, :].rearrange("p (a q n) -> p a n q", a=2, n=SB)
                nc.vector.transpose(dst, src).then_inc(y_turned, 1)

            def y_lo_own(b, i):
                dve.wait_ge(yhi_done, b * CONVS + (i + 1))
                mh, g = i // G, i % G
                nc.vector.tensor_tensor(y_part(y_lo, mh, g), y_turn(i), y_part(y_hi, mh, g).bitcast(F32),
                                        ALU.subtract).then_inc(ylo_own, 1)

            def y_tile(b, i):
                dve.wait_ge(conv_ready, b * CONVS + (i + 1))
                if i >= 2 or not isinstance(b, int):
                    dve.wait_ge(y_turned, b * CONVS + (i - 1))
                term = ctx_all[:, i % G, bass.ds(b * SB, SB)].unsqueeze(1).broadcast_to([P, 64, SB])
                nc.vector.tensor_tensor(y_add[:, i % 2, :].rearrange("p (m n) -> p m n", n=SB),
                                        conv[i % CBANKS][:, :].rearrange("p (m n) -> p m n", n=SB),
                                        term, ALU.add).then_inc(conv_free, 1)
                if i >= 1:
                    y_turned_over(b, i - 1)
                if i == G:
                    y_lo_own(b, G - 1)

            def ax_steps(b):
                dve.wait_ge(ax_half, b + 1)
                nc.vector.tensor_tensor(ax_sum[:, :], rank[0:R, :], ax_sum[:, :], ALU.add).then_inc(ax_summed, 1)
                dve.wait_ge(axhi_done, b * 2 + 2)
                nc.vector.tensor_tensor(ax_st[2 * R:STACK, :], ax_sum[:, :],
                                        ax_st[0:R, :].bitcast(F32), ALU.subtract).then_inc(axlo_done, 1)

            def finish(b, cl):
                dve.wait_ge(tile_done, b * TT + (cl + 1))
                dve.wait_ge(res_ready, b * TT + (cl + 1))
                nc.vector.tensor_tensor(res[:, cl, :], main[cl % 2][:, :], res[:, cl, :],
                                        ALU.add).then_inc(main_free, 1)

            nc.vector.memset(taps[:, :, :], 0.0).then_inc(taps_zero, 1)
            dve.wait_ge(ident_ready, 2)
            nc.vector.tensor_reduce(diag[:, :], ident[:, :].rearrange("p (n r) -> p r n", r=R8), AX.X, ALU.add).then_inc(diag_done, 1)
            dve.wait_ge(gate_in, 16)
            nc.vector.tensor_copy(gate_rep[:, :, :], gate_nat[:, :].unsqueeze(2).broadcast_to([NB, NL, R8])).then_inc(gate_cp, 1)
            dve.wait_ge(diag_done, 1)
            dve.wait_ge(gate_tr, 1)
            nc.vector.tensor_tensor(gmix[:, :, :], diag[:, :].unsqueeze(1).broadcast_to([P, NB, R8]),
                                    rank[:, P:P + NB].unsqueeze(2).broadcast_to([P, NB, R8]), ALU.mult).then_inc(gmix_done, 1)
            dve.wait_ge(cbias_in, 16)
            nc.vector.tensor_copy(bias_rep[:, :].rearrange("g (j l h) -> g j l h", j=J, l=CL),
                                  bias_nat[:, :].rearrange("g (h l) -> g l h", l=CL)
                                  .unsqueeze(1).broadcast_to([G, J, CL, CH])).then_inc(bias_rep_done, 1)
            dve.wait_ge(ctx_tr, 1)
            nc.vector.tensor_copy(cond_t[:, :], rank[:, 0:NS]).then_inc(ctx_cp, 1)
            for g in range(G):
                nc.vector.tensor_copy(
                    cw_rep[:, g, :].rearrange("p (j l h) -> p j l h", j=J, l=CL),
                    rank[:, NS + g * CG:NS + (g + 1) * CG].rearrange("p (h l) -> p l h", l=CL)
                    .unsqueeze(1).broadcast_to([P, J, CL, CH])).then_inc(ctx_cp, 1)
            dve.wait_ge(halo_zero, 2)
            xturn(0, 0)
            xturn(0, 1)
            xlo(0, 0)
            xturn(0, 2)

            def bs_split(h):
                dve.wait_ge(bs_hi, h + 1)
                rows = slice(R, 2 * R)
                nc.vector.tensor_tensor(bs_cols(bs_st[rows, :], h), bs_turned(conv[1 + h][rows, :]),
                                        bs_cols(bs_st[rows, :], h).bitcast(F32), ALU.subtract).then_inc(bs_lo, 1)

            bs_split(0)
            xlo(0, 2)
            xturn(0, 3)
            xlo(0, 3)
            for i in range(POOL_T, 2 * J):
                dve.wait_ge(thi_done, i + 1)
                nc.vector.tensor_tensor(toeplitz(t_lo, i), toeplitz_in(i), toeplitz(t_hi, i).bitcast(F32),
                                        ALU.subtract).then_inc(tlo_done, 1)
            bs_split(1)
            dve.wait_ge(ctx_mm, 1)
            nc.vector.tensor_copy(bias_col[:, :], rank[:, P + NB:P + NB + G]).then_inc(bcol_done, 1)
            dve.wait_ge(bcol_done, 1)
            nc.vector.tensor_tensor(ctx_all[:, :, :], rank[:, 256:256 + G * NS].rearrange("p (g n) -> p g n", g=G),
                                    bias_col[:, :].unsqueeze(2).broadcast_to([P, G, NS]), ALU.add).then_inc(ctx_done, 1)
            xturn(0, 4)
            xturn(0, 5)
            xlo(0, 4)
            xturn(0, 6)

            def as_split(jl):
                dve.wait_ge(as_hi, jl + 1)
                nc.vector.tensor_tensor(ordered(as_st[2 * R:STACK, :], jl), natural(as_rep[2 * R:STACK, :], jl),
                                        ordered(as_st[2 * R:STACK, :], jl).bitcast(F32), ALU.subtract).then_inc(as_lo, 1)

            def be_split(i):
                dve.wait_ge(be_hi, i + 1)
                half = slice((i % 2) * 512, (i % 2 + 1) * 512)
                nc.vector.tensor_tensor(be[64:P, i // 2, half], conv[i % CBANKS][0:NB * R8, :],
                                        be[0:64, i // 2, half].bitcast(F32), ALU.subtract).then_inc(be_lo, 1)

            dve.wait_ge(ctx_done, 1)
            for i in range(CONVS):
                y_tile(0, i)
                if i == 0:
                    xlo(0, 6)
                    xturn(0, 7)
                if i >= 6:
                    as_split(i - 6)
            y_turned_over(0, CONVS - 1)
            be_split(0)
            y_lo_own(0, CONVS - 1)

            def w_lo_own(k):
                dve.wait_ge(whi_done, k + 1)
                nc.vector.tensor_tensor(w_lo[:, k, :], w_raw[:, k, :], w_hi[:, k, :].bitcast(F32),
                                        ALU.subtract).then_inc(wlo_own, 1)

            def w_add(m):
                k, half = m // 2, slice((m % 2) * 512, (m % 2 + 1) * 512)
                dve.wait_ge(kern_in[k // 2], 64)
                dve.wait_ge(w_mm, m + 1)
                nc.vector.tensor_tensor(w_raw[:, k, half], w_bank(m), w_raw[:, k, half], ALU.add).then_inc(w_sum, 1)

            for i in range(1, 2 * RQ):
                if 3 <= i < 6:
                    w_add(i - 3)
                if i == 5:
                    w_add(3)
                be_split(i)
            for m in range(4, 16):
                w_add(m)
            for k in DVE_W:
                w_lo_own(k)
            ax_steps(0)
            with dve.Fori(1, NB) as b:
                finish(b - 1, 0)
                x_steps(b, 0, 3)
                finish(b - 1, 1)
                x_steps(b, 3, 6)
                finish(b - 1, 2)
                x_steps(b, 6, CHUNKS)
                finish(b - 1, 3)
                for i in range(CONVS):
                    y_tile(b, i)
                y_turned_over(b, CONVS - 1)
                y_lo_own(b, CONVS - 1)
                ax_steps(b)
            for cl in range(TT - 1):
                finish(NB - 1, cl)
            dve.wait_ge(res_ready, NB * TT)
            for h in range(2):
                half = slice(h * 512, (h + 1) * 512)
                dve.wait_ge(tile_done, NB * TT + h)
                nc.vector.tensor_tensor(res[:, TT - 1, half], main[(TT - 1) % 2][:, half], res[:, TT - 1, half],
                                        ALU.add).then_inc(main_free, 1)

        @block.tensor
        def _(pe):
            mm = nc.tensor.matmul

            pe.wait_ge(ident_ready, 2)
            pe.wait_ge(gate_cp, 1)
            mm(rank[:, P:P + NB], gate_rep[:, :, :].rearrange("b n r -> b (n r)"), ident[0:NB, 0:NB],
               start=True, stop=True).then_inc(gate_tr, 1)

            def mix_a(k):
                pe.wait_ge(la_ordered, k + 1)
                for q in range(RQ):
                    last = mm(a_out(k)[:, q * 64:(q + 1) * 64], la_ord[:, k, q, :],
                              gmix[:, :, :].rearrange("p b r -> p (b r)"), start=True, stop=True)
                last.then_inc(a_mm, 1)

            pe.wait_ge(gmix_done, 1)
            for k in range(3):
                mix_a(k)
            pe.wait_ge(ctx_in, 32)
            nc.tensor.transpose(rank[:, 0:NS], cond_nat[:, :], ident[0:NS, 0:NS])
            nc.tensor.transpose(rank[:, NS:NS + C], cw_nat[:, :], ident[0:C, 0:C])
            pe.wait_ge(bias_rep_done, 1)
            nc.tensor.transpose(rank[:, P + NB:P + NB + G], bias_rep[:, :], ident[0:G, 0:G]).then_inc(ctx_tr, 1)
            pe.wait_ge(bs_cp, 1)
            for j in range(J):
                last = nc.tensor.transpose(conv[1 + j // 4][0:STACK, (j % 4) * P:(j % 4 + 1) * P],
                                           bs_rep[:, j, :, :].rearrange("p a r -> p (a r)"), ident[:, :])
            last.then_inc(bs_tr, 1)
            mix_a(3)
            mix_a(4)
            pe.wait_ge(ctx_cp, 1 + G)
            for g in range(G):
                last = mm(rank[:, 256 + g * NS:256 + (g + 1) * NS], cw_rep[:, g, :], cond_t[:, :], start=True, stop=True)
            last.then_inc(ctx_mm, 1)
            for k in range(5, KC):
                mix_a(k)

            def convolve(b):
                for i in range(CONVS):
                    mh, g = i // G, i % G
                    if isinstance(b, int) and b == 0:
                        if g == 0:
                            pe.wait_ge(*x_split(0, 4 * mh + 2))
                            pe.wait_ge(*x_split(0, 4 * mh + 3))
                        if 1 <= i < CBANKS:
                            pe.wait_ge(bs_lo, i)
                    elif i == 0:
                        pe.wait_ge(xlo_done, b * CHUNKS + (CHUNKS - len(POOL_X)))
                    before = i - CBANKS if i >= CBANKS else (6, 7, 5)[i] - CONVS
                    pe.wait_ge(conv_free, b * CONVS + (before + 1 + CONVS))
                    n = 0
                    for w in range(2):
                        rows = slice(mh * 64 + w, mh * 64 + w + 64)
                        for lhs, rhs in ((t_hi, x_hi), (t_hi, x_lo), (t_lo, x_hi)):
                            last = mm(conv[i % CBANKS][:, :], lhs[:, w, g, :],
                                      rhs[:, g, rows, :].rearrange("p m n -> p (m n)"), start=n == 0, stop=n == 5)
                            n += 1
                    last.then_inc(conv_ready, 1)

            def turn_b(q):
                if q == 0:
                    pe.wait_ge(lb_ordered, 4)
                if q < 2:
                    pe.wait_ge(a_done, KC)
                else:
                    pe.wait_ge(lbt_done, q - 1)
                for j in range(J):
                    t = nc.tensor.transpose(main[q % 2][:, j * P:(j + 1) * P],
                                            lb_ord[:, j * RQ + q, :, :].rearrange("p n r -> p (n r)"), ident[:, :])
                t.then_inc(lb_tr, 1)

            def mix_b(i):
                pe.wait_ge(lbt_done, i // 2 + 1)
                if i < CBANKS:
                    pe.wait_ge(conv_free, CONVS + (7, 8, 6)[i])
                else:
                    pe.wait_ge(be_lo, i - CBANKS + 1)
                mm(conv[i % CBANKS][0:NB * R8, :], gmix[:, :, :].rearrange("p b r -> p (b r)"),
                   lbt[:, i // 2, (i % 2) * 512:(i % 2 + 1) * 512], start=True, stop=True).then_inc(be_mm, 1)

            def merge(m):
                if m < 4:
                    pe.wait_ge(lbt_done, RQ)
                elif m >= 8:
                    pe.wait_ge(w_sum, m - 3)
                elif m > 4:
                    pe.wait_ge(be_lo, (7, 8, 6)[m - 5])
                mm(w_bank(m), as_st[0:STACK, (m // 2) * P:(m // 2 + 1) * P],
                   bs_st[0:STACK, (m % 2) * 512:(m % 2 + 1) * 512], start=True, stop=True).then_inc(w_mm, 1)

            pe.wait_ge(tlo_pool, POOL_T)
            pe.wait_ge(tlo_done, 2 * J - POOL_T)
            convolve(0)
            turn_b(0)
            turn_b(1)
            for i in range(2 * RQ):
                mix_b(i)
                if i < 2:
                    turn_b(2 + i)
                if i == 2:
                    pe.wait_ge(as_lo, 2)
                if 2 <= i < 6:
                    merge(i - 2)

            def dense(b, cl, k, halves=(0, 1)):
                yh = y_hi[:, (k * CL + cl) * CH:(k * CL + cl + 1) * CH, :].rearrange("p h s -> p (h s)")
                yl = y_lo[:, (k * CL + cl) * CH:(k * CL + cl + 1) * CH, :].rearrange("p h s -> p (h s)")
                for lhs, rhs, first in ((yh, w_hi, True), (yh, w_lo, False), (yl, w_hi, False)):
                    for h in halves:
                        mm(main[cl % 2][:, h * 512:(h + 1) * 512], lhs, rhs[:, k, h * 512:(h + 1) * 512],
                           start=k == 0 and first, stop=False)

            def lowrank(b, cl, halves=(0, 1)):
                for h in halves:
                    last = mm(main[cl % 2][:, h * 512:(h + 1) * 512], ax_st[0:STACK, cl * P:(cl + 1) * P],
                              b_cur[0:STACK, h * 512:(h + 1) * 512], start=False, stop=True)
                last.then_inc(tile_done, 1)

            def with_a(b):
                pe.wait_ge(acur_done, b + 1)
                for kk in range(KC):
                    lhs = a_cur[:, kk, :, :].rearrange("p a r -> p (a r)")
                    for y in (y_hi, y_lo):
                        last = mm(rank[0:2 * R, :], lhs, y[:, kk * 16:(kk + 1) * 16, :].rearrange("p q s -> p (q s)"),
                                  start=kk == 0 and y is y_hi, stop=kk == KC - 1 and y is y_lo)
                last.then_inc(ax_ready, 1)

            def tokens(b):
                first = isinstance(b, int) and b == 0
                pe.wait_ge(*y_split(b, 2))
                pe.wait_ge(*y_split(b, 3))
                pe.wait_ge(main_free, b * TT + 2)
                for k in range(4):
                    if first:
                        for m in ((4, 5, 6, 7), (8, 9), (10, 11), (12, 13, 14, 15))[k]:
                            merge(m)
                        pe.wait_ge(*w_split(k))
                    dense(b, 0, k)
                    dense(b, 1, k)
                pe.wait_ge(*y_split(b, 6))
                pe.wait_ge(*y_split(b, 7))
                if first:
                    pe.wait_ge(w_sum, 2 * KC)
                with_a(b)
                for cl in range(2):
                    for k in range(4, KC):
                        if first and cl == 0:
                            pe.wait_ge(*w_split(k))
                        dense(b, cl, k)
                    if cl == 0:
                        pe.wait_ge(axlo_done, b + 1)
                        pe.wait_ge(b_loaded, b * 48 + 48)
                    lowrank(b, cl)
                for cl in range(2, TT):
                    pe.wait_ge(main_free, b * TT + (cl + 1))
                    last_tile = isinstance(b, int) and b == NB - 1 and cl == TT - 1
                    for halves in (((0,), (1,)) if last_tile else ((0, 1),)):
                        for k in range(KC):
                            dense(b, cl, k, halves)
                        lowrank(b, cl, halves)

            pe.wait_ge(w_sum, 4)
            tokens(0)
            convolve(1)
            with pe.Fori(1, NB - 1) as b:
                tokens(b)
                convolve(b + 1)
            tokens(NB - 1)


_INS = ['x', 'cond_128', 'fside_S_0', 'L0_cond_weight', 'L0_cond_c_weight', 'L0_ffn_gate', 'L0_ffn_kernel',
        'L0_ffn_bias', 'L0_ffn_lora_A', 'L0_ffn_lora_B', 'L0_ffn_lora_A_shared', 'L0_ffn_lora_B_shared']


def kernel(**inputs):
    import concourse.bacc as bacc
    from concourse.bass_utils import run_bass_kernel_spmd

    nc = bacc.Bacc("TRN2", target_bir_lowering=False, num_devices=1)
    arrays, args = {}, []
    for name in _INS:
        a = np.ascontiguousarray(inputs[name])
        arrays[f"in_{name}"] = a
        args.append(nc.dram_tensor(f"in_{name}", a.shape, mybir.dt.from_np(a.dtype), kind="ExternalInput").ap())
    args.append(nc.dram_tensor("out", (NS, C, L), F32, kind="ExternalOutput").ap())
    adaln_ffn(nc, *args)
    r = run_bass_kernel_spmd(nc, [arrays], core_ids=[0])
    return r.results[0]["out"]
```
